# Optimizing a Trainium2 kernel written in Bass

```python
import numpy as np
import jax
import jax.numpy as jnp

def _softmax(x, axis=-1):
    return jax.nn.softmax(x, axis=axis)

def _gelu(x):
    return jax.nn.gelu(x, approximate=True)

def _silu(x):
    return jax.nn.silu(x)

def _sigmoid(x):
    return jax.nn.sigmoid(x)

def _layernorm(x, axis=-1, eps=1e-05):
    m = jnp.mean(x, axis=axis, keepdims=True)
    v = jnp.var(x, axis=axis, keepdims=True)
    return (x - m) / jnp.sqrt(v + eps)

def _scatter_add(tgt, idx, src, axis=0):
    return tgt.at[idx].add(src)

def _segment_sum(src, seg, n):
    return jax.ops.segment_sum(src, seg, n)
kernel_name = 'mk_adaln_attn_ffn_d1_seqx_r4_66250a'

def setup_inputs(seed: int=0):
    np.random.seed(seed)
    _w = jnp.asarray

    def _rec_inputs():
        import jax
        import jax.numpy as jnp
        _rk = jax.random.key(seed)
        x = -0.0002071 + 1 * jax.random.normal(jax.random.fold_in(_rk, 1), (32, 256, 256), jnp.float32)
        _lenS = 256 - jax.random.randint(jax.random.fold_in(_rk, 7), (32,), 0, max(1, 256 // 4) + 1, jnp.int32)
        _lenS2 = 256 - jax.random.randint(jax.random.fold_in(_rk, 8), (32,), 0, max(1, 256 // 4) + 1, jnp.int32)
        cond_8 = jax.random.uniform(jax.random.fold_in(_rk, 11), (32, 8), jnp.float32, 0.0, 0.983423)
        return (x, cond_8)
    x, cond_8 = _rec_inputs()

    def _L0_cond_setup():
        import jax, jax.numpy as jnp
        import numpy as np
        R = 16
        ALPHA = 32.0
        SCALING = ALPHA / R
        key = jax.random.key(seed)
        ks = jax.random.split(key, 6)
        B, T, C, O, E = (16, 375, 256, 256, 8)
        x = jax.random.normal(ks[0], (B, T, C), dtype=jnp.float32)
        w = jax.random.uniform(ks[1], (B, E), dtype=jnp.float32)
        W_base = jax.random.normal(ks[2], (O, C), dtype=jnp.float32) * 0.02
        b_base = jax.random.normal(ks[3], (O,), dtype=jnp.float32) * 0.02
        As = jax.random.normal(ks[4], (E, R, C), dtype=jnp.float32) * 0.02
        Bs = jax.random.normal(ks[5], (E, O, R), dtype=jnp.float32) * 0.02
        return {'x': x, 'w': w, 'W_base': W_base, 'b_base': b_base, 'As': As, 'Bs': Bs}
    _L0_cond_all = _L0_cond_setup()
    _L0_cond_in = {k: v for k, v in _L0_cond_all.items() if k in ('W_base', 'b_base', 'As', 'Bs')}
    del _L0_cond_all

    def _L0_attn_setup():
        import jax, jax.numpy as jnp
        import numpy as np
        HIDDEN = 256
        NHEADS = 16
        HEAD_DIM = HIDDEN // NHEADS
        CONV_K = 4
        EPS = 1e-06

        def _short_conv(x, w):
            K = w.shape[-1]
            L = x.shape[1]
            xp = jnp.pad(x, ((0, 0), (K - 1, 0), (0, 0)))
            y = jnp.zeros_like(x)
            for k in range(K):
                y = y + xp[:, k:k + L, :] * w[:, k]
            return y

        def _l2norm(x):
            n = jnp.sqrt(jnp.sum(x * x, axis=-1, keepdims=True))
            return x / jnp.maximum(n, EPS)

        def _delta_rule(q, k, v, beta):
            b, h, l, dk = q.shape
            dv = v.shape[-1]
            q = q * dk ** (-0.5)
            S0 = jnp.zeros((b, h, dk, dv), dtype=v.dtype)

            def step(S, inp):
                q_t, k_t, v_t, b_t = inp
                v_new = (v_t - jnp.einsum('bhd,bhdm->bhm', k_t, S)) * b_t[..., None]
                S = S + jnp.einsum('bhd,bhm->bhdm', k_t, v_new)
                o_t = jnp.einsum('bhd,bhdm->bhm', q_t, S)
                return (S, o_t)
            ql, kl, vl = (t.transpose(2, 0, 1, 3) for t in (q, k, v))
            bl = beta.transpose(2, 0, 1)
            S, o = jax.lax.scan(step, S0, (ql, kl, vl, bl))
            return (o.transpose(1, 2, 0, 3), S)

        def _reference_tuple_inner(x, Wq, Wk, Wv, Wb, Wo, conv_q, conv_k, conv_v, o_norm_w):
            b, l, _ = x.shape
            q = x @ Wq.T
            k = x @ Wk.T
            v = x @ Wv.T
            beta = jax.nn.sigmoid(x @ Wb.T)
            q = jax.nn.silu(_short_conv(q, conv_q))
            k = jax.nn.silu(_short_conv(k, conv_k))
            v = jax.nn.silu(_short_conv(v, conv_v))

            def to_heads(t):
                return t.reshape(b, l, NHEADS, HEAD_DIM).transpose(0, 2, 1, 3)
            q, k, v = (to_heads(q), to_heads(k), to_heads(v))
            beta = beta.transpose(0, 2, 1)
            q = _l2norm(q)
            k = _l2norm(k)
            o, S = _delta_rule(q, k, v, beta)
            o = o * jax.lax.rsqrt(jnp.mean(o * o, axis=-1, keepdims=True) + EPS) * o_norm_w
            out = o.transpose(0, 2, 1, 3).reshape(b, l, HIDDEN) @ Wo.T
            return (out, S)
        key = jax.random.key(seed)
        ks = jax.random.split(key, 10)
        b, l = (4, 256)
        init = 0.02
        return {'x': jax.random.normal(ks[0], (b, l, HIDDEN), dtype=jnp.float32), 'Wq': jax.random.normal(ks[1], (HIDDEN, HIDDEN), dtype=jnp.float32) * init, 'Wk': jax.random.normal(ks[2], (HIDDEN, HIDDEN), dtype=jnp.float32) * init, 'Wv': jax.random.normal(ks[3], (HIDDEN, HIDDEN), dtype=jnp.float32) * init, 'Wb': jax.random.normal(ks[4], (NHEADS, HIDDEN), dtype=jnp.float32) * init, 'Wo': jax.random.normal(ks[5], (HIDDEN, HIDDEN), dtype=jnp.float32) * init, 'conv_q': jax.random.normal(ks[6], (HIDDEN, CONV_K), dtype=jnp.float32) * 0.3, 'conv_k': jax.random.normal(ks[7], (HIDDEN, CONV_K), dtype=jnp.float32) * 0.3, 'conv_v': jax.random.normal(ks[8], (HIDDEN, CONV_K), dtype=jnp.float32) * 0.3, 'o_norm_w': jnp.ones((HEAD_DIM,), dtype=jnp.float32)}
    _L0_attn_all = _L0_attn_setup()
    _L0_attn_in = {k: v for k, v in _L0_attn_all.items() if k in ('Wq', 'Wk', 'Wv', 'Wb', 'Wo', 'conv_q', 'conv_k', 'conv_v', 'o_norm_w')}
    del _L0_attn_all

    def _L0_cond2_setup():
        import jax, jax.numpy as jnp
        import numpy as np
        key = jax.random.key(seed)
        k1, k2, k3, k4, k5 = jax.random.split(key, 5)
        B, N, T, O, G = (32, 64, 256, 256, 8)
        x = jax.random.normal(k1, (B, N, T), dtype=jnp.float32)
        y = jax.random.uniform(k2, (B, G), dtype=jnp.float32)
        weight = jax.random.normal(k3, (G, O, T), dtype=jnp.float32) * (1.0 / np.sqrt(T))
        mask = jax.random.uniform(k4, (O, T), dtype=jnp.float32)
        bias = jax.random.normal(k5, (O,), dtype=jnp.float32)
        return {'x': x, 'y': y, 'weight': weight, 'mask': mask, 'bias': bias}
    _L0_cond2_all = _L0_cond2_setup()
    _L0_cond2_in = {k: v for k, v in _L0_cond2_all.items() if k in ('weight', 'mask', 'bias')}
    del _L0_cond2_all

    def _L0_ffn_setup():
        import jax, jax.numpy as jnp
        import numpy as np
        import math
        BETA = 0.9
        THRESHOLD = 1.0
        NUM_STEPS = 5
        ALPHA = 2.0

        @jax.custom_vjp
        def spike_fn(u):
            return (u > 0).astype(u.dtype)

        def _spike_fwd(u):
            return (spike_fn(u), u)

        def _spike_bwd(u, g):
            s = jnp.pi / 2.0 * ALPHA * u
            return (g * (ALPHA / 2.0) / (1.0 + s * s),)
        spike_fn.defvjp(_spike_fwd, _spike_bwd)
        key = jax.random.key(seed)
        k1, k2, k3 = jax.random.split(key, 3)
        n_embd = 256
        x = jax.random.normal(k1, (4, 512, n_embd), dtype=jnp.float32)
        W_fc = jax.random.normal(k2, (4 * n_embd, n_embd), dtype=jnp.float32) / math.sqrt(n_embd)
        W_proj = jax.random.normal(k3, (n_embd, 4 * n_embd), dtype=jnp.float32) / math.sqrt(4 * n_embd)
        return {'x': x, 'W_fc': W_fc, 'W_proj': W_proj}
    _L0_ffn_all = _L0_ffn_setup()
    _L0_ffn_in = {k: v for k, v in _L0_ffn_all.items() if k in ('W_fc', 'W_proj')}
    del _L0_ffn_all
    return {'x': x, 'cond_8': cond_8, 'L0_cond_W_base': _L0_cond_in['W_base'], 'L0_cond_b_base': _L0_cond_in['b_base'], 'L0_cond_As': _L0_cond_in['As'], 'L0_cond_Bs': _L0_cond_in['Bs'], 'L0_attn_Wq': _L0_attn_in['Wq'], 'L0_attn_Wk': _L0_attn_in['Wk'], 'L0_attn_Wv': _L0_attn_in['Wv'], 'L0_attn_Wb': _L0_attn_in['Wb'], 'L0_attn_Wo': _L0_attn_in['Wo'], 'L0_attn_conv_q': _L0_attn_in['conv_q'], 'L0_attn_conv_k': _L0_attn_in['conv_k'], 'L0_attn_conv_v': _L0_attn_in['conv_v'], 'L0_attn_o_norm_w': _L0_attn_in['o_norm_w'], 'L0_cond2_weight': _L0_cond2_in['weight'], 'L0_cond2_mask': _L0_cond2_in['mask'], 'L0_cond2_bias': _L0_cond2_in['bias'], 'L0_ffn_W_fc': _L0_ffn_in['W_fc'], 'L0_ffn_W_proj': _L0_ffn_in['W_proj']}

def reference(x, cond_8, L0_cond_W_base, L0_cond_b_base, L0_cond_As, L0_cond_Bs, L0_attn_Wq, L0_attn_Wk, L0_attn_Wv, L0_attn_Wb, L0_attn_Wo, L0_attn_conv_q, L0_attn_conv_k, L0_attn_conv_v, L0_attn_o_norm_w, L0_cond2_weight, L0_cond2_mask, L0_cond2_bias, L0_ffn_W_fc, L0_ffn_W_proj):
    import jax
    import jax.numpy as jnp

    def _L0_cond_ref(x, w, W_base, b_base, As, Bs):
        import jax, jax.numpy as jnp
        import numpy as np
        R = 16
        ALPHA = 32.0
        SCALING = ALPHA / R
        out = jnp.einsum('btc,oc->bto', x, W_base) + b_base
        h = jnp.einsum('btc,erc->bter', x, As)
        lora = jnp.einsum('bter,eor,be->bto', h, Bs, w)
        return out + lora * SCALING

    def _L0_attn_ref(x, Wq, Wk, Wv, Wb, Wo, conv_q, conv_k, conv_v, o_norm_w):
        import jax, jax.numpy as jnp
        import numpy as np
        HIDDEN = 256
        NHEADS = 16
        HEAD_DIM = HIDDEN // NHEADS
        CONV_K = 4
        EPS = 1e-06

        def _short_conv(x, w):
            K = w.shape[-1]
            L = x.shape[1]
            xp = jnp.pad(x, ((0, 0), (K - 1, 0), (0, 0)))
            y = jnp.zeros_like(x)
            for k in range(K):
                y = y + xp[:, k:k + L, :] * w[:, k]
            return y

        def _l2norm(x):
            n = jnp.sqrt(jnp.sum(x * x, axis=-1, keepdims=True))
            return x / jnp.maximum(n, EPS)

        def _delta_rule(q, k, v, beta):
            b, h, l, dk = q.shape
            dv = v.shape[-1]
            q = q * dk ** (-0.5)
            S0 = jnp.zeros((b, h, dk, dv), dtype=v.dtype)

            def step(S, inp):
                q_t, k_t, v_t, b_t = inp
                v_new = (v_t - jnp.einsum('bhd,bhdm->bhm', k_t, S)) * b_t[..., None]
                S = S + jnp.einsum('bhd,bhm->bhdm', k_t, v_new)
                o_t = jnp.einsum('bhd,bhdm->bhm', q_t, S)
                return (S, o_t)
            ql, kl, vl = (t.transpose(2, 0, 1, 3) for t in (q, k, v))
            bl = beta.transpose(2, 0, 1)
            S, o = jax.lax.scan(step, S0, (ql, kl, vl, bl))
            return (o.transpose(1, 2, 0, 3), S)

        def _reference_tuple_inner(x, Wq, Wk, Wv, Wb, Wo, conv_q, conv_k, conv_v, o_norm_w):
            b, l, _ = x.shape
            q = x @ Wq.T
            k = x @ Wk.T
            v = x @ Wv.T
            beta = jax.nn.sigmoid(x @ Wb.T)
            q = jax.nn.silu(_short_conv(q, conv_q))
            k = jax.nn.silu(_short_conv(k, conv_k))
            v = jax.nn.silu(_short_conv(v, conv_v))

            def to_heads(t):
                return t.reshape(b, l, NHEADS, HEAD_DIM).transpose(0, 2, 1, 3)
            q, k, v = (to_heads(q), to_heads(k), to_heads(v))
            beta = beta.transpose(0, 2, 1)
            q = _l2norm(q)
            k = _l2norm(k)
            o, S = _delta_rule(q, k, v, beta)
            o = o * jax.lax.rsqrt(jnp.mean(o * o, axis=-1, keepdims=True) + EPS) * o_norm_w
            out = o.transpose(0, 2, 1, 3).reshape(b, l, HIDDEN) @ Wo.T
            return (out, S)
        return _reference_tuple_inner(x, Wq, Wk, Wv, Wb, Wo, conv_q, conv_k, conv_v, o_norm_w)[0]

    def _L0_cond2_ref(x, y, weight, mask, bias):
        import jax, jax.numpy as jnp
        import numpy as np
        masked_w = weight * mask[None, :, :]
        w_bot = jnp.einsum('bg,got->bot', y, masked_w)
        return jnp.einsum('bnt,bot->bno', x, w_bot) + bias

    def _L0_ffn_ref(x, W_fc, W_proj):
        import jax, jax.numpy as jnp
        import numpy as np
        import math
        BETA = 0.9
        THRESHOLD = 1.0
        NUM_STEPS = 5
        ALPHA = 2.0

        @jax.custom_vjp
        def spike_fn(u):
            return (u > 0).astype(u.dtype)

        def _spike_fwd(u):
            return (spike_fn(u), u)

        def _spike_bwd(u, g):
            s = jnp.pi / 2.0 * ALPHA * u
            return (g * (ALPHA / 2.0) / (1.0 + s * s),)
        spike_fn.defvjp(_spike_fwd, _spike_bwd)
        h = jnp.square(jax.nn.relu(jnp.einsum('bsd,fd->bsf', x, W_fc)))
        y = jnp.einsum('bsf,df->bsd', h, W_proj)

        def step(mem, _):
            reset = jax.lax.stop_gradient(spike_fn(mem - THRESHOLD))
            mem_new = BETA * mem + y - reset * THRESHOLD
            spk = spike_fn(mem_new - THRESHOLD)
            return (mem_new, spk)
        mem0 = jnp.zeros_like(y)
        _, spks = jax.lax.scan(step, mem0, None, length=NUM_STEPS)
        return jnp.sum(spks, axis=0) / NUM_STEPS
    x = x + _L0_attn_ref(_L0_cond_ref(x, cond_8, L0_cond_W_base, L0_cond_b_base, L0_cond_As, L0_cond_Bs), L0_attn_Wq, L0_attn_Wk, L0_attn_Wv, L0_attn_Wb, L0_attn_Wo, L0_attn_conv_q, L0_attn_conv_k, L0_attn_conv_v, L0_attn_o_norm_w)
    x = x + _L0_ffn_ref(_L0_cond2_ref(x, cond_8, L0_cond2_weight, L0_cond2_mask, L0_cond2_bias), L0_ffn_W_fc, L0_ffn_W_proj)
    return x

_drawn_inputs = setup_inputs


def setup_inputs(seed=0):
    import zlib

    import numpy as np

    out = dict(_drawn_inputs(seed))
    spreads = {'L0_attn_o_norm_w': (1.0, 0.2)}
    factors = {}
    for name, (base, spread) in spreads.items():
        noise = np.random.default_rng([zlib.crc32(name.encode()), seed]).standard_normal(out[name].shape)
        drawn = base * np.exp(spread * noise) if base else spread * noise
        out[name] = jnp.asarray(drawn.astype(out[name].dtype))
    for name, factor in factors.items():
        out[name] = (out[name] * factor).astype(out[name].dtype)
    return out
```

```python
from contextlib import ExitStack, contextmanager

import numpy as np

import concourse.bass as bass
from concourse import mybir

F32 = mybir.dt.float32
ALU = mybir.AluOpType
ACT = mybir.ActivationFunctionType
AX_X = mybir.AxisListType.X
P = 128

ALPHA, RANK = 32.0, 16
L2_EPS, RMS_EPS = 1e-6, 1e-6
BETA, THRESHOLD, NUM_STEPS = 0.9, 1.0, 5


def spike_thresholds():
    f = np.float32

    def count(y):
        mem, spikes = f(0), 0
        for _ in range(NUM_STEPS):
            reset = f(mem - f(THRESHOLD) > 0)
            mem = f(f(f(BETA) * mem) + y) - reset * f(THRESHOLD)
            spikes += int(mem - f(THRESHOLD) > 0)
        return spikes

    edges = []
    for n in range(1, NUM_STEPS + 1):
        low, high = int(f(0.125).view(np.uint32)), int(f(8.0).view(np.uint32))
        while high - low > 1:
            mid = (low + high) // 2
            if count(np.uint32(mid).view(np.float32)) >= n:
                high = mid
            else:
                low = mid
        edges.append(float(np.uint32(low).view(np.float32)))
    return edges


def adaln_attention_ffn(nc, x, cond, W_base, b_base, As, Bs, Wq, Wk, Wv, Wb, Wo, conv_q, conv_k,
                        conv_v, o_norm_w, weight2, mask2, bias2, W_fc, W_proj, out):
    B, T, C = x.shape
    H = Wb.shape[0]
    D = C // H
    E = cond.shape[1]
    F = W_fc.shape[0]
    TAPS = conv_q.shape[1]
    CB = C // P
    TB = T // P
    FB = F // P
    GB = P // H
    GROUPS = B // GB
    WIN = 64
    WPG = T // WIN
    SLOTS = GROUPS * WPG
    PER = GB // WPG
    UN = 16
    LEAD, FOLLOW = WPG, WPG + 1
    OPG = P // E
    OG = C // OPG
    OQ = 4
    assert PER == 2 and D * H == C and E * RANK == P

    SEGMENTS = [(0, 1, 1, 0, 1, 0), (1, FOLLOW, 1, 0, 1, 1), (FOLLOW, FOLLOW + 1, 1, 1, 1, 1),
                (FOLLOW + 1, SLOTS - LEAD, 1, 1, 1, 1),
                (SLOTS - LEAD, SLOTS - 1, 0, 1, 1, 1), (SLOTS - 1, SLOTS + 1, 0, 1, 0, 1),
                (SLOTS + 1, SLOTS + FOLLOW, 0, 1, 0, 0)]

    @contextmanager
    def slots(eng, first, last):
        if last - first == 1:
            yield first
        else:
            with eng.Fori(first, last) as s:
                yield s

    qkv_d = nc.dram_tensor("qkv_scratch", [3, B, C, T], F32).ap()
    beta_d = nc.dram_tensor("beta_scratch", [B * H, T], F32).ap()
    o_d = nc.dram_tensor("o_scratch", [B * H, D, T], F32).ap()
    map_d = nc.dram_tensor("map_scratch", [B, C, C], F32).ap()

    with ExitStack() as ctx:
        def sb(name, shape):
            return ctx.enter_context(nc.sbuf_tensor(name, shape, F32))

        def sem(name):
            return ctx.enter_context(nc.semaphore(name))

        ident = sb("ident", [P, P])
        fifth = sb("fifth", [P, P])
        ones = sb("ones", [P, P])
        WbaseT = sb("WbaseT", [P, CB, C])
        WqkvT = sb("WqkvT", [P, 3, CB, C])
        WoT = sb("WoT", [P, CB, C])
        WbT = sb("WbT", [P, CB, H])
        AsT = sb("AsT", [P, CB, P])
        BsT = sb("BsT", [P, C])
        WfcT = sb("WfcT", [P, CB, F])
        WprojT = sb("WprojT", [P, FB, C])
        taps = sb("taps", [P, 3, CB, TAPS])
        diag = sb("diag", [P, 3, CB, TAPS, P])
        bcol = sb("bcol", [P, CB])
        b2col = sb("b2col", [P, CB])
        normcol = sb("normcol", [P, 1])
        condn = sb("condn", [B, E])
        cond_wide = sb("cond_wide", [B, E, RANK])
        cond_rows = sb("cond_rows", [P, B])
        pick = sb("pick", [P, OPG])
        natural = sb("natural", [P, 8192])
        off = [0]

        def nat(n):
            off[0] += n
            return natural[:, off[0] - n:off[0]]

        n_base = nat(CB * C).rearrange("p (a c) -> p a c", a=CB)
        n_qkv = [nat(CB * C).rearrange("p (a c) -> p a c", a=CB) for _ in range(3)]
        n_o = nat(CB * C).rearrange("p (a c) -> p a c", a=CB)
        n_As = nat(C)
        n_Bs = nat(CB * P).rearrange("p (a e) -> p a e", a=CB)
        n_Wb = nat(C)
        n_fc = nat(FB * C).rearrange("p (a c) -> p a c", a=FB)
        n_proj = nat(CB * F).rearrange("p (a f) -> p a f", a=CB)
        map_w = natural[:, 0:OG * C].rearrange("p (a t) -> p a t", a=OG)
        map_m = natural[:, OG * C:2 * OG * C].rearrange("p (a t) -> p a t", a=OG)
        pick_cond = sb("pick_cond", [P, OPG, B])
        map_st = sb("map_st", [P, 2, B, OQ, OPG])

        x_tok = sb("x_tok", [P, 2, TB, C])
        xT = sb("xT", [P, CB, T])
        loraT = sb("loraT", [P, T])
        yT = sb("yT", [P, CB, T])
        pre = sb("pre", [P, 3, CB, TAPS - 1 + T])
        act = sb("act", [P, 2, 3, CB, T])
        beta_sb = sb("beta_sb", [H, 2, T])
        qkv_w = sb("qkv_w", [P, 2, 3, D, WIN])
        beta_w = sb("beta_w", [P, 2, WIN])
        o_w = sb("o_w", [P, 2, D, WIN])
        o_out = sb("o_out", [P, D, WIN])
        state = sb("state", [P, D, D])
        prod_k = sb("prod_k", [P, D, D])
        prod_q = sb("prod_q", [P, D, D])
        outer = sb("outer", [P, D, D])
        kS = sb("kS", [P, D])
        wv = sb("wv", [P, D])
        sqr = sb("sqr", [P, D, WIN])
        ss = sb("ss", [P, 2, WIN])
        so = sb("so", [P, WIN])
        root = sb("root", [P, 2, WIN])
        rooto = sb("rooto", [P, WIN])
        rinv = sb("rinv", [P, 2, 2, WIN])
        tmp = sb("tmp", [P, 2, WIN])
        rk_beta = sb("rk_beta", [P, 2, WIN])
        rq_o = sb("rq_o", [P, WIN])
        rinvo = sb("rinvo", [P, WIN])
        tmpo = sb("tmpo", [P, WIN])
        xf_tok = sb("xf_tok", [P, 2, TB, C])
        oT = sb("oT", [P, 2, CB, T])
        mapb = sb("mapb", [P, 2, CB, C])
        x2T = sb("x2T", [P, CB, T])
        zT = sb("zT", [P, CB, T])
        hid = sb("hid", [P, FB, T])
        drive = sb("drive", [P, CB, T])
        over = sb("over", [P, CB, T])
        count = sb("count", [P, CB, T])
        out_sb = sb("out_sb", [P, 2, TB, C])

        proj_ps = ctx.enter_context(nc.psum_tensor("proj_ps", [P, 4, 512], F32))
        fwd_ps = ctx.enter_context(nc.psum_tensor("fwd_ps", [P, 4, 512], F32))

        w_loaded, c_loaded, map_loaded, mask_loaded = map(sem, ("w_loaded", "c_loaded", "map_loaded", "mask_loaded"))
        const_ready, ident_ready = sem("const_ready"), sem("ident_ready")
        setup_full, setup_free = sem("setup_full"), sem("setup_free")
        map_full, map_free = sem("map_full"), sem("map_free")
        map_masked, pick_ready = sem("map_masked"), sem("pick_ready")
        map_stored = [sem("map_stored0"), sem("map_stored1")]
        diag_ready, pad_ready, wide_ready = sem("diag_ready"), sem("pad_ready"), sem("wide_ready")
        x_loaded = [sem("x_loaded0"), sem("x_loaded1")]
        proj_full, proj_free = sem("proj_full"), sem("proj_free")
        qkv_stored = [sem("qkv_stored0"), sem("qkv_stored1")]
        win_loaded, win_done = sem("win_loaded"), sem("win_done")
        ss_ready, root_ready = sem("ss_ready"), sem("root_ready")
        so_ready, rooto_ready = sem("so_ready"), sem("rooto_ready")
        o_ready, o_stored = sem("o_ready"), sem("o_stored")
        kprod_done, kS_done, w_done, outer_done, state_done = map(
            sem, ("kprod_done", "kS_done", "w_done", "outer_done", "state_done"))
        qprod_done, qS_done = sem("qprod_done"), sem("qS_done")
        dve_seq, state_clear = sem("dve_seq"), sem("state_clear")
        groups_begun, compares_begun = sem("groups_begun"), sem("compares_begun")
        xf_loaded = [sem("xf_loaded0"), sem("xf_loaded1")]
        fwd_full, fwd_free = sem("fwd_full"), sem("fwd_free")
        hid_squared, over_ready, count_done = sem("hid_squared"), sem("over_ready"), sem("count_done")
        out_stored = [sem("out_stored0"), sem("out_stored1")]

        PROJ, FWD = 10, 8

        block = ctx.enter_context(nc.Block())

        jobs = []
        def job(blocks, dest, kind="copy"):
            jobs.append((blocks, dest, kind))

        for a in range(CB):
            job([n_base[:, o, a * P:(a + 1) * P] for o in range(CB)], WbaseT[:, a, :])
            for n in range(3):
                job([n_qkv[n][:, o, a * P:(a + 1) * P] for o in range(CB)], WqkvT[:, n, a, :])
            job([n_o[:, o, a * P:(a + 1) * P] for o in range(CB)], WoT[:, a, :], "norm")
            for h in range(FB // 4):
                job([n_fc[:, 4 * h + o, a * P:(a + 1) * P] for o in range(4)],
                    WfcT[:, a, h * 512:(h + 1) * 512])
        for f in range(FB):
            job([n_proj[:, o, f * P:(f + 1) * P] for o in range(CB)], WprojT[:, f, :])
        job([n_As[:, a * P:(a + 1) * P] for a in range(CB)], AsT[:, :, :])
        job([n_Bs[:, a, :] for a in range(CB)], BsT[:, :], "scaling")
        for a in range(CB):
            job([n_Wb[0:H, a * P:(a + 1) * P]], WbT[:, a, :])
        JOBS = len(jobs) + 1

        @block.sync
        def _(sp):
            def natural_rows(dst, src, a):
                sp.dma_start(dst, src.rearrange("(a p) c -> p a c", a=a)).then_inc(w_loaded, 16)

            natural_rows(n_base, W_base, CB)
            for n, w in enumerate((Wq, Wk, Wv)):
                natural_rows(n_qkv[n], w, CB)
            natural_rows(n_o, Wo, CB)
            natural_rows(n_fc, W_fc, FB)
            natural_rows(n_proj, W_proj, CB)
            sp.dma_start(n_As, As.rearrange("e r c -> (e r) c")).then_inc(w_loaded, 16)
            for a in range(CB):
                sp.dma_start(n_Bs[:, a, :].rearrange("p (e r) -> p e r", e=E),
                             Bs[:, a * P:(a + 1) * P, :].rearrange("e o r -> o e r")).then_inc(w_loaded, 16)
            sp.dma_start(n_Wb[0:H, :], Wb).then_inc(w_loaded, 16)
            for n, w in enumerate((conv_q, conv_k, conv_v)):
                sp.dma_start(taps[:, n, :, :], w.rearrange("(a p) k -> p a k", a=CB)).then_inc(c_loaded, 16)
            with nc.allow_non_contiguous_dma(reason="a few vectors as columns"):
                sp.dma_start(bcol[:, :], b_base.rearrange("(a p) -> p a", a=CB)).then_inc(c_loaded, 16)
                sp.dma_start(b2col[:, :], bias2.rearrange("(a p) -> p a", a=CB)).then_inc(c_loaded, 16)
                for h in range(P // D):
                    sp.dma_start(normcol[h * D:(h + 1) * D, :],
                                 o_norm_w.rearrange("(d a) -> d a", a=1)).then_inc(c_loaded, 16)
            sp.dma_start(condn[:, :], cond).then_inc(c_loaded, 16)

            def load_x(n, par):
                sp.dma_start(x_tok[:, par, :, :], x[bass.ds(n, 1)].rearrange("b (a p) c -> p (b a) c", a=TB)
                             ).then_inc(x_loaded[par], 16)

            def store_qkv(n, par, pair):
                sp.wait_ge(proj_free, PROJ * (n + 1))
                for w in range(3):
                    sp.dma_start(qkv_d[w, bass.ds(n, 1)].rearrange("b (a p) t -> p (b a) t", a=CB),
                                 act[:, par, w, :, :]).then_inc(qkv_stored[par], 16)
                sp.dma_start(beta_d[bass.ds(n * H, H), :], beta_sb[:, par, :]).then_inc(qkv_stored[par], 16)

            def project_loads(pair, first=False):
                for par in range(2):
                    n = 2 * pair + par
                    if not first:
                        sp.wait_ge(proj_full, PROJ * (n - 2) + 1)
                    load_x(n, par)

            def window_load(s):
                group, w, par = s // WPG, s % WPG, s % 2
                for n in range(3):
                    sp.dma_start(
                        qkv_w[:, bass.ds(par, 1), n, :, :].rearrange("p o d t -> p (o d) t"),
                        qkv_d[n].rearrange("b (h d) t -> (b h) d t", d=D)[bass.ds(group * P, P), :, bass.ds(w * WIN, WIN)]
                    ).then_inc(win_loaded, 16)
                sp.dma_start(beta_w[:, bass.ds(par, 1), :].rearrange("p o t -> p (o t)"),
                             beta_d[bass.ds(group * P, P), bass.ds(w * WIN, WIN)]).then_inc(win_loaded, 16)

            def forward_loads(pair, first=False):
                for par in range(2):
                    m = 2 * pair + par
                    if not first:
                        sp.wait_ge(fwd_full, FWD * (m - 2) + 2)
                    sp.dma_start(xf_tok[:, par, :, :], x[bass.ds(m, 1)].rearrange("b (a p) c -> p (b a) c", a=TB)
                                 ).then_inc(xf_loaded[par], 16)
                    sp.dma_start(mapb[:, par, :, :], map_d[bass.ds(m, 1)].rearrange("b (a p) o -> p (b a) o", a=CB)
                                 ).then_inc(xf_loaded[par], 16)
                    sp.dma_start(oT[:, par, :, :],
                                 o_d[bass.ds(m * H, H)].rearrange("(a h) d t -> (h d) a t", a=CB)
                                 ).then_inc(xf_loaded[par], 16)

            def store_out(m, par):
                sp.wait_ge(fwd_free, FWD * (m + 1))
                sp.dma_start(out[bass.ds(m, 1)].rearrange("b (a p) c -> p (b a) c", a=TB), out_sb[:, par, :, :]
                             ).then_inc(out_stored[par], 16)

            project_loads(0, first=True)
            sp.wait_ge(setup_full, JOBS)
            for g in range(E):
                sp.dma_start(map_w[g * OPG:(g + 1) * OPG, :, :],
                             weight2[g].rearrange("(a o) t -> o a t", o=OPG)).then_inc(map_loaded, 16)
                sp.dma_start(map_m[g * OPG:(g + 1) * OPG, :, :],
                             mask2.rearrange("(a o) t -> o a t", o=OPG)).then_inc(mask_loaded, 16)
            for par in range(2):
                store_qkv(par, par, 0)
            with sp.Fori(1, LEAD) as pair:
                project_loads(pair)
                for par in range(2):
                    store_qkv(2 * pair + par, par, pair)
            for par in range(2):
                sp.wait_ge(qkv_stored[par], 64 * LEAD)
            window_load(0)

            chunk = 0
            for a in range(CB):
                for oq in range(OG // OQ):
                    sp.wait_ge(map_free, OQ * (chunk + 1))
                    sp.dma_start(
                        map_d[:, a * P:(a + 1) * P, oq * OQ * OPG:(oq + 1) * OQ * OPG].rearrange("b t o -> t b o"),
                        map_st[:, chunk % 2, :, :, :].rearrange("t b a o -> t b (a o)")
                    ).then_inc(map_stored[chunk % 2], 16)
                    chunk += 1

            for par in range(2):
                sp.wait_ge(map_stored[par], 16 * (chunk // 2))

            for first, last, project, forward, nxt, prev in SEGMENTS:
                with slots(sp, first, last) as s:
                    if forward:
                        sp.wait_ge(o_stored, 16 * (s - 1) if first <= SLOTS else 16 * SLOTS)
                        forward_loads(s - FOLLOW, first=(first == FOLLOW))
                    if project:
                        project_loads(s + LEAD)
                    for par in range(2):
                        if project:
                            store_qkv(2 * (s + LEAD) + par, par, s + LEAD)
                        if forward:
                            store_out(2 * (s - FOLLOW) + par, par)
                    if nxt:
                        for par in range(2):
                            if project:
                                sp.wait_ge(qkv_stored[par], 64 * (s + LEAD + 1))
                        if prev:
                            sp.wait_ge(win_done, s)
                        window_load(s + 1)
                    if prev:
                        sp.wait_ge(o_ready, s)
                        group, w = (s - 1) // WPG, (s - 1) % WPG
                        sp.dma_start(o_d[bass.ds(group * P, P), :, bass.ds(w * WIN, WIN)], o_out[:, :, :]
                                     ).then_inc(o_stored, 16)
            for par in range(2):
                sp.wait_ge(out_stored[par], 16 * (B // 2))
                sp.wait_ge(qkv_stored[par], 64 * (B // 2))
            sp.wait_ge(o_stored, 16 * SLOTS)

        @block.gpsimd
        def _(pool):
            pool.memset(ones[:, :], 1.0).then_inc(const_ready, 1)
            pool.wait_ge(const_ready, 1)
            pool.affine_select(out=ident[:, :], in_=ones[:, :], compare_op=ALU.is_equal, fill=0.0, base=0,
                               pattern=[[-1, P]], channel_multiplier=1).then_inc(ident_ready, 1)
            pool.wait_ge(ident_ready, 1)
            pool.tensor_scalar(fifth[:, :], ident[:, :], 1.0 / NUM_STEPS, None, ALU.mult).then_inc(const_ready, 1)
            pool.memset(pre[:, :, :, 0:TAPS - 1], 0.0).then_inc(pad_ready, 1)
            pool.wait_ge(map_loaded, 16 * E)
            pool.wait_ge(mask_loaded, 16 * E)
            pool.tensor_tensor(map_w, map_w, map_m, ALU.mult).then_inc(map_masked, 1)
            edges = spike_thresholds()

            def forward(m):
                for k in range(FB // 2):
                    pool.wait_ge(fwd_free, FWD * m + 3 + k)
                    h = hid[:, 2 * k:2 * k + 2, :]
                    pool.tensor_tensor(h, h, h, ALU.mult).then_inc(hid_squared, 1)
                pool.wait_ge(fwd_free, FWD * m + 7)
                pool.sem_inc(compares_begun, 1)
                n_over, n_count = (NUM_STEPS - 1) * m, NUM_STEPS * m
                pool.tensor_scalar(count[:, :, :], drive[:, :, :], edges[0], None, ALU.is_gt).then_inc(count_done, 1)
                for n in range(1, NUM_STEPS):
                    pool.tensor_scalar(over[:, :, :], drive[:, :, :], edges[n], None, ALU.is_gt
                                       ).then_inc(over_ready, 1)
                    pool.wait_ge(over_ready, n_over + n)
                    pool.wait_ge(count_done, n_count + n)
                    pool.tensor_tensor(count[:, :, :], count[:, :, :], over[:, :, :], ALU.add).then_inc(count_done, 1)
                    pool.wait_ge(count_done, n_count + n + 1)
                    pool.sem_inc(compares_begun, 1)

            with pool.Fori(0, B) as m:
                forward(m)

        @block.vector
        def _(dve):
            seq = [0]

            def then(ins):
                seq[0] += 1
                ins.then_inc(dve_seq, 1)
                dve.wait_ge(dve_seq, seq[0])

            dve.wait_ge(ident_ready, 1)
            then(dve.tensor_reduce(pick[:, :], ident[:, :].rearrange("p (g o) -> p o g", g=E), AX_X, ALU.add))
            dve.wait_ge(c_loaded, 16 * (6 + P // D))
            dve.tensor_copy(cond_wide[:, :, :], condn[:, :].rearrange("b (e u) -> b e u", u=1).broadcast_to([B, E, RANK])
                            ).then_inc(wide_ready, 1)
            for n in range(3):
                for a in range(CB):
                    for k in range(TAPS):
                        dve.tensor_scalar(diag[:, n, a, k, :], ident[:, :], taps[:, n, a, k:k + 1], None,
                                          ALU.mult).then_inc(diag_ready, 1)
            dve.wait_ge(setup_free, JOBS)
            dve.tensor_tensor(pick_cond[:, :, :], pick[:, :].rearrange("p (o u) -> p o u", u=1).broadcast_to([P, OPG, B]),
                              cond_rows[:, :].rearrange("p (u b) -> p u b", u=1).broadcast_to([P, OPG, B]),
                              ALU.mult).then_inc(pick_ready, 1)

            base = seq[0]

            def step_sem(part):
                at = [0]

                def go(ins):
                    at[0] += 1
                    ins.then_inc(dve_seq, 1)
                    dve.wait_ge(dve_seq, part + at[0])
                return go, at

            def norms_sum(go, s, par):
                dve.wait_ge(win_loaded, 64 * (s + 1))
                for n in range(2):
                    w = qkv_w[:, par, n, :, :]
                    go(dve.tensor_tensor(sqr[:, :, :], w, w, ALU.mult))
                    go(dve.tensor_reduce(ss[:, n, :], sqr[:, :, :].rearrange("p d t -> p t d"), AX_X, ALU.add))
                dve.tensor_scalar(ss[:, :, :], ss[:, :, :], L2_EPS * L2_EPS, None, ALU.max).then_inc(ss_ready, 1)

            def norms_inverse(go, s, par):
                dve.wait_ge(root_ready, s + 1)
                r = rinv[:, par, :, :]
                go(dve.reciprocal(r, root[:, :, :]))
                go(dve.tensor_tensor(tmp[:, :, :], r, r, ALU.mult))
                go(dve.tensor_tensor(tmp[:, :, :], tmp[:, :, :], ss[:, :, :], ALU.mult))
                go(dve.tensor_scalar(tmp[:, :, :], tmp[:, :, :], -0.5, 1.5, ALU.mult, ALU.add))
                go(dve.tensor_tensor(r, r, tmp[:, :, :], ALU.mult))
                go(dve.tensor_tensor(rk_beta[:, par, :], rinv[:, par, 1, :], beta_w[:, par, :], ALU.mult))

            def output_sum(go, s, par):
                go(dve.tensor_scalar(rq_o[:, :], rinv[:, par, 0, :], D ** -0.5, None, ALU.mult))
                go(dve.tensor_tensor(sqr[:, :, :], o_w[:, par, :, :], o_w[:, par, :, :], ALU.mult))
                go(dve.tensor_reduce(so[:, :], sqr[:, :, :].rearrange("p d t -> p t d"), AX_X, ALU.add))
                go(dve.tensor_tensor(so[:, :], so[:, :], rq_o[:, :], ALU.mult))
                go(dve.tensor_tensor(so[:, :], so[:, :], rq_o[:, :], ALU.mult))
                dve.tensor_scalar(so[:, :], so[:, :], 1.0 / D, RMS_EPS, ALU.mult, ALU.add).then_inc(so_ready, 1)

            def output_scale(go, s, par):
                dve.wait_ge(rooto_ready, s + 1)
                go(dve.reciprocal(rinvo[:, :], rooto[:, :]))
                go(dve.tensor_tensor(tmpo[:, :], rinvo[:, :], rinvo[:, :], ALU.mult))
                go(dve.tensor_tensor(tmpo[:, :], tmpo[:, :], so[:, :], ALU.mult))
                go(dve.tensor_scalar(tmpo[:, :], tmpo[:, :], -0.5, 1.5, ALU.mult, ALU.add))
                go(dve.tensor_tensor(rinvo[:, :], rinvo[:, :], tmpo[:, :], ALU.mult))
                go(dve.tensor_tensor(rinvo[:, :], rinvo[:, :], rq_o[:, :], ALU.mult))
                if not (isinstance(s, int) and s == 0):
                    dve.wait_ge(o_stored, 16 * s)
                dve.tensor_tensor(o_out[:, :, :], o_w[:, par, :, :],
                                  rinvo[:, :].rearrange("p (u t) -> p u t", u=1).broadcast_to([P, D, WIN]),
                                  ALU.mult).then_inc(o_ready, 1)

            def wide(v):
                return v.rearrange("p (m u) -> p m u", u=1).broadcast_to([P, D, D])

            def over_rows(v):
                return v.rearrange("p d u -> p u d").broadcast_to([P, D, D])

            def recurrence(s, par, half):
                q, k, v = (qkv_w[:, par, n] for n in range(3))
                blocks = WIN // UN // 2
                with dve.Fori(half * blocks, (half + 1) * blocks) as blk:
                    t0 = blk * UN
                    for u in range(UN):
                        t = t0 + u
                        at = s * WIN + t
                        one = bass.ds(t, 1)
                        dve.tensor_tensor(prod_k[:, :, :], state[:, :, :], over_rows(k[:, :, one]), ALU.mult
                                          ).then_inc(kprod_done, 1)
                        if u:
                            query(q, t - 1, at - 1)
                        dve.wait_ge(kprod_done, at + 1)
                        dve.tensor_reduce(kS[:, :], prod_k[:, :, :], AX_X, ALU.add).then_inc(kS_done, 1)
                        if u:
                            answer(par, t - 1, at - 1)
                        dve.wait_ge(kS_done, at + 1)
                        dve.scalar_tensor_tensor(out=wv[:, :], in0=kS[:, :], scalar=rinv[:, par, 1, one],
                                                 in1=v[:, :, one].rearrange("p m u -> p (m u)"),
                                                 op0=ALU.mult, op1=ALU.subtract).then_inc(w_done, 1)
                        dve.wait_ge(w_done, at + 1)
                        dve.scalar_tensor_tensor(out=outer[:, :, :], in0=wide(wv[:, :]), scalar=rk_beta[:, par, one],
                                                 in1=over_rows(k[:, :, one]), op0=ALU.mult, op1=ALU.mult
                                                 ).then_inc(outer_done, 1)
                        dve.wait_ge(outer_done, at + 1)
                        dve.tensor_tensor(state[:, :, :], state[:, :, :], outer[:, :, :], ALU.subtract
                                          ).then_inc(state_done, 1)
                        dve.wait_ge(state_done, at + 1)
                    query(q, t0 + (UN - 1), s * WIN + t0 + (UN - 1))
                    answer(par, t0 + (UN - 1), s * WIN + t0 + (UN - 1))

            def query(q, t, at):
                dve.tensor_tensor(prod_q[:, :, :], state[:, :, :], over_rows(q[:, :, bass.ds(t, 1)]), ALU.mult
                                  ).then_inc(qprod_done, 1)

            def answer(par, t, at):
                dve.wait_ge(qprod_done, at + 1)
                dve.tensor_reduce(o_w[:, par, :, bass.ds(t, 1)].rearrange("p m u -> p (m u)"), prod_q[:, :, :], AX_X, ALU.add
                                  ).then_inc(qS_done, 1)

            PER_NEXT, PER_PREV = 4 + 6, 5 + 6

            def window(s, w, group, first=False, last=False):
                par = w % 2
                part = base + PER_NEXT + s * (PER_NEXT + PER_PREV) - (0 if first else PER_PREV)
                go, at = step_sem(part)
                if w == 0:
                    dve.memset(state[:, :, :], 0.0).then_inc(state_clear, 1)
                    dve.wait_ge(state_clear, group + 1)
                    dve.sem_inc(groups_begun, 1)
                recurrence(s, par, 0)
                if not first:
                    dve.wait_ge(qS_done, s * WIN)
                    output_sum(go, s - 1, 1 - par)
                if not last:
                    norms_sum(go, s + 1, 1 - par)
                recurrence(s, par, 1)
                if not last:
                    norms_inverse(go, s + 1, 1 - par)
                if not first:
                    output_scale(go, s - 1, 1 - par)
                dve.wait_ge(qS_done, (s + 1) * WIN)
                dve.sem_inc(win_done, 1)

            go, _ = step_sem(base)
            norms_sum(go, 0, 0)
            norms_inverse(go, 0, 0)
            window(0, 0, 0, first=True)
            with dve.Fori(0, GROUPS - 1) as i:
                for w in range(1, WPG + 1):
                    window(WPG * i + w, w % WPG, i + w // WPG)
            for w in range(1, WPG):
                s = WPG * (GROUPS - 1) + w
                window(s, w, GROUPS - 1, last=(s == SLOTS - 1))
            go, _ = step_sem(base + PER_NEXT * SLOTS + PER_PREV * (SLOTS - 1))
            output_sum(go, SLOTS - 1, (SLOTS - 1) % 2)
            output_scale(go, SLOTS - 1, (SLOTS - 1) % 2)

        @block.scalar
        def _(act_e):
            act_e.wait_ge(c_loaded, 16 * (6 + P // D))
            for j, (blocks, dest, kind) in enumerate(jobs):
                act_e.wait_ge(setup_full, j + 1)
                width = sum(b.shape[0] for b in blocks)
                src = proj_ps[:, j % 4, 0:width]
                if len(dest.shape) == 3:
                    src = src.rearrange("p (a e) -> p a e", a=dest.shape[1])
                scale = {"copy": 1.0, "norm": normcol[:, 0:1], "scaling": ALPHA / RANK}[kind]
                act_e.activation(dest, src, ACT.Copy, scale=scale).then_inc(setup_free, 1)
            act_e.wait_ge(setup_full, JOBS)
            act_e.activation(cond_rows[:, :], proj_ps[:, (JOBS - 1) % 4, 0:B], ACT.Copy).then_inc(setup_free, 1)

            def project(n, par, first=False):
                ring = [(PROJ * par + k) % 4 for k in range(PROJ)]

                def full(k):
                    act_e.wait_ge(proj_full, PROJ * n + k + 1)

                def bank(k, a=2):
                    return proj_ps[:, ring[k], :].rearrange("p (a t) -> p a t", a=a)

                full(0)
                act_e.activation(xT[:, :, :], bank(0), ACT.Copy).then_inc(proj_free, 1)
                full(1)
                act_e.activation(loraT[:, :], proj_ps[:, ring[1], 0:T], ACT.Copy, scale=cond_rows[:, bass.ds(n, 1)]
                                 ).then_inc(proj_free, 1)
                full(2)
                for a in range(CB):
                    last = act_e.activation(yT[:, a, :], bank(2)[:, a, :], ACT.Identity, bias=bcol[:, a:a + 1])
                last.then_inc(proj_free, 1)
                if first:
                    act_e.wait_ge(pad_ready, 1)
                for w in range(3):
                    full(3 + w)
                    act_e.activation(pre[:, w, :, TAPS - 1:], bank(3 + w), ACT.Copy).then_inc(proj_free, 1)
                if not first:
                    act_e.wait_ge(qkv_stored[par], 32 * (n - par))
                full(6)
                act_e.activation(beta_sb[:, par, :], proj_ps[0:H, ring[6], 0:T], ACT.Sigmoid).then_inc(proj_free, 1)
                for w in range(3):
                    full(7 + w)
                    last = act_e.activation(act[:, par, w, :, :], bank(7 + w), ACT.Silu)
                    last.then_inc(proj_free, 1)

            def fwd_bank(k):
                return fwd_ps[:, k % 4, :].rearrange("p (a t) -> p a t", a=2)

            def forward_main(m):
                def full(k):
                    act_e.wait_ge(fwd_full, FWD * m + k + 1)

                full(0)
                act_e.activation(x2T[:, :, :], fwd_bank(0), ACT.Copy).then_inc(fwd_free, 1)
                full(1)
                for a in range(CB):
                    last = act_e.activation(zT[:, a, :], fwd_bank(1)[:, a, :], ACT.Identity, bias=b2col[:, a:a + 1])
                last.then_inc(fwd_free, 1)
                for k in range(FB // 2):
                    full(2 + k)
                    act_e.activation(hid[:, 2 * k:2 * k + 2, :], fwd_bank(2 + k), ACT.Relu).then_inc(fwd_free, 1)
                full(6)
                act_e.activation(drive[:, :, :], fwd_bank(6), ACT.Copy).then_inc(fwd_free, 1)

            def forward_tail(m, par, first=False):
                act_e.wait_ge(fwd_full, FWD * m + 8)
                if not first:
                    act_e.wait_ge(out_stored[par], 8 * (m - par))
                act_e.activation(out_sb[:, par, :, :], fwd_bank(7), ACT.Copy).then_inc(fwd_free, 1)

            act_e.wait_ge(setup_free, JOBS)
            for par in range(2):
                project(par, par, first=True)
            with act_e.Fori(1, LEAD) as pair:
                for par in range(2):
                    project(2 * pair + par, par)

            def root_next(s):
                act_e.wait_ge(ss_ready, s + 1)
                act_e.activation(root[:, :, :], ss[:, :, :], ACT.Sqrt).then_inc(root_ready, 1)

            def root_prev(s):
                act_e.wait_ge(so_ready, s + 1)
                act_e.activation(rooto[:, :], so[:, :], ACT.Sqrt).then_inc(rooto_ready, 1)

            root_next(0)

            use, chunk = 0, 0
            for a in range(CB):
                for oq in range(OG // OQ):
                    if chunk >= 2:
                        act_e.wait_ge(map_stored[chunk % 2], 16 * (chunk // 2))
                    for k in range(OQ):
                        act_e.wait_ge(map_full, use + 1)
                        last = act_e.activation(map_st[:, chunk % 2, :, k, :],
                                                fwd_ps[:, use % 4, :].rearrange("p (o b) -> p b o", o=OPG), ACT.Copy)
                        last.then_inc(map_free, 1)
                        use += 1
                    chunk += 1

            for first, last, project_, forward, nxt, prev in SEGMENTS:
                with slots(act_e, first, last) as s:
                    for par in range(2):
                        m = 2 * (s - FOLLOW) + par
                        if forward:
                            forward_main(m)
                        if project_:
                            project(2 * (s + LEAD) + par, par)
                        if forward:
                            forward_tail(m, par, first=(first == FOLLOW))
                    if prev:
                        root_prev(s - 1)
                    if nxt:
                        root_next(s + 1)

        @block.tensor
        def _(pe):
            pe.wait_ge(ident_ready, 1)
            pe.wait_ge(w_loaded, 16 * 11)
            for j, (blocks, dest, kind) in enumerate(jobs):
                if j >= 4:
                    pe.wait_ge(setup_free, j - 3)
                at = 0
                for b in blocks:
                    rows = b.shape[0]
                    last = pe.transpose(proj_ps[:, j % 4, at:at + rows], b, ident[0:rows, 0:rows])
                    at += rows
                last.then_inc(setup_full, 1)
            pe.wait_ge(setup_free, JOBS - 4)
            pe.wait_ge(wide_ready, 1)
            pe.matmul(proj_ps[:, (JOBS - 1) % 4, 0:B], cond_wide[:, :, :].rearrange("b e r -> b (e r)"),
                      ident[0:B, 0:B], start=True, stop=True).then_inc(setup_full, 1)
            pe.wait_ge(setup_free, JOBS)
            pe.wait_ge(diag_ready, 3 * CB * TAPS)

            def project(n, par, first=False):
                ring = [(PROJ * par + k) % 4 for k in range(PROJ)]

                def free(k):
                    if not (first and PROJ * par + k < 4):
                        pe.wait_ge(proj_free, PROJ * n + k - 3)

                def read(k):
                    pe.wait_ge(proj_free, PROJ * n + k + 1)

                def bank(k, a):
                    return proj_ps[:, ring[k], a * T:(a + 1) * T]

                pe.wait_ge(x_loaded[par], 8 * (n - par) + 16)
                free(0)
                for a in range(CB):
                    for tb in range(TB):
                        last = pe.transpose(proj_ps[:, ring[0], a * T + tb * P:a * T + (tb + 1) * P],
                                            x_tok[:, par, tb, a * P:(a + 1) * P], ident[:, :])
                last.then_inc(proj_full, 1)
                free(1)
                read(0)
                for c in range(CB):
                    last = pe.matmul(bank(1, 0), AsT[:, c, :], xT[:, c, :], start=(c == 0), stop=(c == CB - 1))
                last.then_inc(proj_full, 1)
                free(2)
                for a in range(CB):
                    for c in range(CB):
                        pe.matmul(bank(2, a), WbaseT[:, c, a * P:(a + 1) * P], xT[:, c, :], start=(c == 0), stop=False)
                    if a == 0:
                        read(1)
                    last = pe.matmul(bank(2, a), BsT[:, a * P:(a + 1) * P], loraT[:, :], start=False, stop=True)
                last.then_inc(proj_full, 1)
                read(2)
                for w in range(3):
                    free(3 + w)
                    for a in range(CB):
                        for c in range(CB):
                            last = pe.matmul(bank(3 + w, a), WqkvT[:, w, c, a * P:(a + 1) * P], yT[:, c, :],
                                             start=(c == 0), stop=(c == CB - 1))
                    last.then_inc(proj_full, 1)
                free(6)
                for c in range(CB):
                    last = pe.matmul(proj_ps[0:H, ring[6], 0:T], WbT[:, c, :], yT[:, c, :],
                                     start=(c == 0), stop=(c == CB - 1))
                last.then_inc(proj_full, 1)
                for w in range(3):
                    free(7 + w)
                    read(3 + w)
                    for a in range(CB):
                        for k in range(TAPS):
                            last = pe.matmul(bank(7 + w, a), diag[:, w, a, k, :], pre[:, w, a, k:k + T],
                                             start=(k == 0), stop=(k == TAPS - 1))
                    last.then_inc(proj_full, 1)

            def fwd_out(k, a):
                return fwd_ps[:, k % 4, a * T:(a + 1) * T]

            def forward_main(m, par):
                def free(k):
                    if k >= 3:
                        pe.wait_ge(fwd_free, FWD * m + k - 3)

                def read(k):
                    pe.wait_ge(fwd_free, FWD * m + k + 1)

                pe.wait_ge(xf_loaded[par], 24 * (m - par) + 48)
                for a in range(CB):
                    for c in range(CB):
                        pe.matmul(fwd_out(0, a), WoT[:, c, a * P:(a + 1) * P], oT[:, par, c, :], start=(c == 0), stop=False,
                                  skip_group_check=True)
                    for tb in range(TB):
                        last = pe.matmul(fwd_ps[:, 0, a * T + tb * P:a * T + (tb + 1) * P],
                                         xf_tok[:, par, tb, a * P:(a + 1) * P], ident[:, :], start=False, stop=True,
                                         skip_group_check=True)
                last.then_inc(fwd_full, 1)
                read(0)
                for a in range(CB):
                    for c in range(CB):
                        last = pe.matmul(fwd_out(1, a), mapb[:, par, c, a * P:(a + 1) * P], x2T[:, c, :],
                                         start=(c == 0), stop=(c == CB - 1))
                last.then_inc(fwd_full, 1)
                read(1)
                for k in range(FB // 2):
                    free(2 + k)
                    for a in range(2):
                        f = 2 * k + a
                        for c in range(CB):
                            last = pe.matmul(fwd_out(2 + k, a), WfcT[:, c, f * P:(f + 1) * P], zT[:, c, :],
                                             start=(c == 0), stop=(c == CB - 1))
                    last.then_inc(fwd_full, 1)
                free(6)
                for a in range(CB):
                    for f in range(FB):
                        if a == 0 and f % 2 == 0:
                            pe.wait_ge(hid_squared, (FB // 2) * m + f // 2 + 1)
                        last = pe.matmul(fwd_out(6, a), WprojT[:, f, a * P:(a + 1) * P], hid[:, f, :],
                                         start=(f == 0), stop=(f == FB - 1))
                last.then_inc(fwd_full, 1)

            def forward_tail(m):
                pe.wait_ge(fwd_free, FWD * m + 4)
                pe.wait_ge(count_done, NUM_STEPS * (m + 1))
                for tb in range(TB):
                    for a in range(CB):
                        o = fwd_ps[:, 3, tb * C + a * P:tb * C + (a + 1) * P]
                        pe.matmul(o, x2T[:, a, tb * P:(tb + 1) * P], ident[:, :], start=True, stop=False)
                        last = pe.matmul(o, count[:, a, tb * P:(tb + 1) * P], fifth[:, :], start=False, stop=True)
                last.then_inc(fwd_full, 1)

            for par in range(2):
                project(par, par, first=True)
            with pe.Fori(1, LEAD) as pair:
                for par in range(2):
                    project(2 * pair + par, par)

            pe.wait_ge(map_masked, 1)
            pe.wait_ge(pick_ready, 1)
            use = 0
            for a in range(CB):
                for og in range(OG):
                    if use >= 4:
                        pe.wait_ge(map_free, use - 3)
                    pe.matmul(fwd_ps[:, use % 4, :], map_w[:, og, a * P:(a + 1) * P], pick_cond[:, :, :],
                              start=True, stop=True).then_inc(map_full, 1)
                    use += 1
            pe.wait_ge(map_free, use)
            pe.wait_ge(const_ready, 2)

            for first, last_, project_, forward, nxt, prev in SEGMENTS:
                with slots(pe, first, last_) as s:
                    for par in range(2):
                        m = 2 * (s - FOLLOW) + par
                        if forward:
                            forward_main(m, par)
                        if project_:
                            project(2 * (s + LEAD) + par, par)
                        if forward:
                            forward_tail(m)


INS = ['x', 'cond_8', 'L0_cond_W_base', 'L0_cond_b_base', 'L0_cond_As', 'L0_cond_Bs', 'L0_attn_Wq', 'L0_attn_Wk',
       'L0_attn_Wv', 'L0_attn_Wb', 'L0_attn_Wo', 'L0_attn_conv_q', 'L0_attn_conv_k', 'L0_attn_conv_v',
       'L0_attn_o_norm_w', 'L0_cond2_weight', 'L0_cond2_mask', 'L0_cond2_bias', 'L0_ffn_W_fc', 'L0_ffn_W_proj']


def kernel(**inputs):
    import numpy as _np
    import concourse.bacc as _bacc
    from concourse import mybir as _mybir
    from concourse.bass_utils import run_bass_kernel_spmd as _run

    nc = _bacc.Bacc("TRN2", target_bir_lowering=False, num_devices=1)
    arrays, args = {}, []
    for name in INS:
        a = _np.ascontiguousarray(inputs[name])
        arrays[f"in_{name}"] = a
        args.append(nc.dram_tensor(f"in_{name}", a.shape, _mybir.dt.from_np(a.dtype), kind="ExternalInput").ap())
    out = nc.dram_tensor("out", inputs["x"].shape, _mybir.dt.float32, kind="ExternalOutput").ap()
    adaln_attention_ffn(nc, *args, out)
    r = _run(nc, [arrays], core_ids=[0])
    return r.results[0]["out"]
```

```python
from contextlib import ExitStack, contextmanager

import numpy as np

import concourse.bass as bass
from concourse import mybir

F32 = mybir.dt.float32
ALU = mybir.AluOpType
ACT = mybir.ActivationFunctionType
AX_X = mybir.AxisListType.X
P = 128

ALPHA, RANK = 32.0, 16
L2_EPS, RMS_EPS = 1e-6, 1e-6
BETA, THRESHOLD, NUM_STEPS = 0.9, 1.0, 5


def spike_thresholds():
    f = np.float32

    def count(y):
        mem, spikes = f(0), 0
        for _ in range(NUM_STEPS):
            reset = f(mem - f(THRESHOLD) > 0)
            mem = f(f(f(BETA) * mem) + y) - reset * f(THRESHOLD)
            spikes += int(mem - f(THRESHOLD) > 0)
        return spikes

    edges = []
    for n in range(1, NUM_STEPS + 1):
        low, high = int(f(0.125).view(np.uint32)), int(f(8.0).view(np.uint32))
        while high - low > 1:
            mid = (low + high) // 2
            if count(np.uint32(mid).view(np.float32)) >= n:
                high = mid
            else:
                low = mid
        edges.append(float(np.uint32(low).view(np.float32)))
    return edges


def adaln_attention_ffn(nc, x, cond, W_base, b_base, As, Bs, Wq, Wk, Wv, Wb, Wo, conv_q, conv_k,
                        conv_v, o_norm_w, weight2, mask2, bias2, W_fc, W_proj, out):
    B, T, C = x.shape
    H = Wb.shape[0]
    D = C // H
    E = cond.shape[1]
    F = W_fc.shape[0]
    TAPS = conv_q.shape[1]
    CB = C // P
    FB = F // P
    HB = P // D
    GB = P // H
    GROUPS = B // GB
    WIN = 64
    WPG = T // WIN
    SLOTS = GROUPS * WPG
    BC = 2 * CB
    UPG = 2 * WPG
    RING = 8
    MH = 2
    DM = D // MH
    LEAD, FOLLOW = 2, 2
    OPG = P // E
    OG = C // OPG
    OQ = 4
    assert T == 2 * P and D * H == C and E * RANK == P and WIN % (4 * RING) == 0

    SEGMENTS = [(0, 1, "pxwn"), (1, FOLLOW, "pxwnu"), (FOLLOW, FOLLOW + 1, "pxfwnu"),
                (FOLLOW + 1, SLOTS - LEAD - 1, "pxfwnu"), (SLOTS - LEAD - 1, SLOTS - LEAD, "pfwnu"),
                (SLOTS - LEAD, SLOTS - 1, "fwnu"), (SLOTS - 1, SLOTS, "fwu"), (SLOTS, SLOTS + 1, "fu"),
                (SLOTS + 1, SLOTS + FOLLOW, "f")]

    @contextmanager
    def slots(eng, first, last):
        if last - first == 1:
            yield first
        else:
            with eng.Fori(first, last) as s:
                yield s

    qkv_d = nc.dram_tensor("qkv_scratch", [3, B, C, T], F32).ap()
    beta_d = nc.dram_tensor("beta_scratch", [B * H, T], F32).ap()
    u_d = nc.dram_tensor("u_scratch", [B * H, D, T], F32).ap()
    s_d = nc.dram_tensor("state_scratch", [SLOTS, P, D, D], F32).ap()
    map_d = nc.dram_tensor("map_scratch", [B, C, C], F32).ap()

    with ExitStack() as ctx:
        def sb(name, shape):
            return ctx.enter_context(nc.sbuf_tensor(name, shape, F32))

        def sem(name):
            return ctx.enter_context(nc.semaphore(name))

        ident = sb("ident", [P, P])
        block_ones = sb("block_ones", [P, P])
        block_mean = sb("block_mean", [P, P])
        WbaseT = sb("WbaseT", [P, CB, C])
        WqkvT = sb("WqkvT", [P, 3, CB, C])
        WoT = sb("WoT", [P, CB, C])
        WbT = sb("WbT", [P, CB, H])
        AsT = sb("AsT", [P, CB, P])
        BsT = sb("BsT", [P, C])
        WfcT = sb("WfcT", [P, CB, F])
        WprojT = sb("WprojT", [P, FB, C])
        taps = sb("taps", [P, 3, CB, TAPS])
        diag = sb("diag", [P, 3, CB, TAPS, P])
        bcol = sb("bcol", [P, CB])
        b2col = sb("b2col", [P, CB])
        normcol = sb("normcol", [P, 1])
        condn = sb("condn", [B, E])
        cond_rows = sb("cond_rows", [P, B])
        cond_units = sb("cond_units", [P, GROUPS, 2, GB])
        pick = sb("pick", [P, OPG])

        region = sb("region", [P, 8192])
        region_2 = sb("region_2", [P, 4096])

        def carve(tensor):
            at = [0]

            def take(n):
                at[0] += n
                return tensor[:, at[0] - n:at[0]]
            return take

        nat = carve(region)
        n_base = nat(CB * C).rearrange("p (a c) -> p a c", a=CB)
        n_qkv = [nat(CB * C).rearrange("p (a c) -> p a c", a=CB) for _ in range(3)]
        n_o = nat(CB * C).rearrange("p (a c) -> p a c", a=CB)
        n_As = nat(C)
        n_Bs = nat(CB * P).rearrange("p (a e) -> p a e", a=CB)
        n_Wb = nat(C)
        n_fc = nat(FB * C).rearrange("p (a c) -> p a c", a=FB)
        n_proj = nat(CB * F).rearrange("p (a f) -> p a f", a=CB)
        map_w = region[:, 0:OG * C].rearrange("p (a t) -> p a t", a=OG)
        map_m = region[:, OG * C:2 * OG * C].rearrange("p (a t) -> p a t", a=OG)
        map_st = region_2[:, :].rearrange("p (i b k o) -> p i b k o", i=2, b=B, k=OQ)
        late = carve(region)
        PAD = P + D
        u_pad = late(BC * HB * PAD).rearrange("p (a x) -> p a x", a=BC)
        hid = late(FB * 2 * P).rearrange("p (f b t) -> p f b t", f=FB, b=2)
        x2T = late(2 * BC * P).rearrange("p (i b a t) -> p i b a t", i=2, b=2, a=CB)
        qsq = late(BC * P)
        late_2 = carve(region_2)
        qm = late_2(2 * 4 * P).rearrange("p (i h t) -> p i h t", i=2, h=4)
        pm = late_2(2 * 4 * P).rearrange("p (i h t) -> p i h t", i=2, h=4)
        drive = late_2(2 * BC * P).rearrange("p (i x) -> p i x", i=2)
        total = late_2(2 * BC * P).rearrange("p (i b a t) -> p i b a t", i=2, b=2, a=CB)

        x_tok = sb("x_tok", [P, 2, 2, C])
        xT = sb("xT", [P, 2, CB, P])
        loraT = sb("loraT", [P, 2, P])
        yT = sb("yT", [P, 2, CB, P])
        pre = sb("pre", [P, 3 * BC, TAPS - 1 + P])
        carry = sb("carry", [P, UPG + 4, 3 * BC, TAPS - 1])
        act = sb("act", [P, 2, 3, BC, P])
        beta_sb = sb("beta_sb", [H, 2, 2, P])
        kv_w = sb("kv_w", [P, 2, 2, D, WIN])
        beta_w = sb("beta_w", [P, 2, WIN])
        w_all = sb("w_all", [P, D, WIN])
        u_out = sb("u_out", [P, D, WIN])
        state = sb("state", [P, D, D])
        dump = sb("dump", [P, D, D])
        prod_ring = sb("prod_ring", [P, RING, D, D + 1])
        sqr = prod_ring[:, :, :, :].rearrange("p r m x -> p (r m x)")[:, 0:D * WIN].rearrange("p (d t) -> p d t", d=D)
        kb = sb("kb", [P, D, WIN])
        outer = sb("outer", [P, D, D])
        ss = sb("ss", [P, WIN])
        root = sb("root", [P, WIN])
        rinv = sb("rinv", [P, 2, WIN])
        tmp = sb("tmp", [P, WIN])
        rk_beta = sb("rk_beta", [P, 2, WIN])
        xf_tok = sb("xf_tok", [P, 2, 2, C])
        q_f = sb("q_f", [P, 2, BC, P])
        k_f = sb("k_f", [P, 2, BC, P])
        u_f = sb("u_f", [P, 2, BC, P])
        s0_f = sb("s0_f", [P, 2, BC, D])
        mapb = sb("mapb", [P, 2, BC, C])
        s0_block = sb("s0_block", [P, BC, HB, D])
        osq = sb("osq", [P, BC * P])
        ones, half_block = osq[:, 0:P], osq[:, P:2 * P]
        cond_wide = osq[0:B, 2 * P:3 * P].rearrange("b (e r) -> b e r", e=E)
        over = osq
        guard = sb("guard", [P, BC * P])
        pick_cond = guard[:, :].rearrange("p (o b) -> p o b", o=OPG)
        count = guard
        o_f = sb("o_f", [P, 2, 2, CB, P])
        scale_f = sb("scale_f", [P, 2, BC * P])
        zT = sb("zT", [P, 2, CB, P])
        out_sb = sb("out_sb", [P, 2, 2, C])

        proj_ps = ctx.enter_context(nc.psum_tensor("proj_ps", [P, 4, 512], F32))
        fwd_ps = ctx.enter_context(nc.psum_tensor("fwd_ps", [P, 4, 512], F32))

        w_loaded, c_loaded, map_loaded, mask_loaded = map(sem, ("w_loaded", "c_loaded", "map_loaded", "mask_loaded"))
        const_ready, ident_ready = sem("const_ready"), sem("ident_ready")
        block_ready = sem("block_ready")
        guard_ready, pm_ready, square_ready = sem("guard_ready"), sem("pm_ready"), sem("square_ready")
        setup_full, setup_free = sem("setup_full"), sem("setup_free")
        map_full, map_free = sem("map_full"), sem("map_free")
        map_masked, pick_ready = sem("map_masked"), sem("pick_ready")
        map_stored = [sem("map_stored0"), sem("map_stored1")]
        diag_ready, wide_ready, pad_ready = sem("diag_ready"), sem("wide_ready"), sem("pad_ready")
        x_loaded = [sem("x_loaded0"), sem("x_loaded1")]
        proj_full, proj_free = sem("proj_full"), sem("proj_free")
        head_ready, carry_saved = sem("head_ready"), sem("carry_saved")
        qkv_stored = [sem("qkv_stored0"), sem("qkv_stored1")]
        win_loaded, win_done = sem("win_loaded"), sem("win_done")
        ss_ready, root_ready = sem("ss_ready"), sem("root_ready")
        u_ready, u_stored = sem("u_ready"), sem("u_stored")
        dump_ready, s_stored = sem("dump_ready"), sem("s_stored")
        v_placed, kprod_done, w_done, outer_done, state_done = map(
            sem, ("v_placed", "kprod_done", "w_done", "outer_done", "state_done"))
        dve_seq, state_clear = sem("dve_seq"), sem("state_clear")
        windows_begun, pool_turns, sp_turns = sem("windows_begun"), sem("pool_turns"), sem("sp_turns")
        f_loaded = [sem("f_loaded0"), sem("f_loaded1")]
        fwd_full, fwd_free = sem("fwd_full"), sem("fwd_free")
        att_full, att_free = sem("att_full"), sem("att_free")
        s0_ready, qsq_ready, qm_ready = sem("s0_ready"), sem("qsq_ready"), sem("qm_ready")
        norm_root, norm_inverse, o_ready = sem("norm_root"), sem("norm_inverse"), sem("o_ready")
        over_ready, rate_ready = sem("over_ready"), sem("rate_ready")
        hid_squared, count_done, total_ready = sem("hid_squared"), sem("count_done"), sem("total_ready")
        out_stored = [sem("out_stored0"), sem("out_stored1")]

        PROJ, FWD = 10, 20
        GRAMS = BC * HB // 4
        ATT = GRAMS + 2
        R_U, R_O = (0, 2), (1, 3)
        R_MAIN, R_TAIL = (4, 11), (18, 19)
        F_DMAS = 6

        block = ctx.enter_context(nc.Block())

        jobs = []

        def job(blocks, dest, kind="copy"):
            jobs.append((blocks, dest, kind))

        job([n_As[:, a * P:(a + 1) * P] for a in range(CB)], AsT[:, :, :])
        job([n_Bs[:, a, :] for a in range(CB)], BsT[:, :], "scaling")
        for a in range(CB):
            job([n_Wb[0:H, a * P:(a + 1) * P]], WbT[:, a, :])
        for a in range(CB):
            job([n_base[:, o, a * P:(a + 1) * P] for o in range(CB)], WbaseT[:, a, :])
            for n in range(3):
                job([n_qkv[n][:, o, a * P:(a + 1) * P] for o in range(CB)], WqkvT[:, n, a, :])
            job([n_o[:, o, a * P:(a + 1) * P] for o in range(CB)], WoT[:, a, :], "norm")
            for h in range(FB // 4):
                job([n_fc[:, 4 * h + o, a * P:(a + 1) * P] for o in range(4)],
                    WfcT[:, a, h * 512:(h + 1) * 512])
        for f in range(FB):
            job([n_proj[:, o, f * P:(f + 1) * P] for o in range(CB)], WprojT[:, f, :])
        JOBS = len(jobs) + 1

        def batch_of(idx, par):
            return (idx // WPG) * GB + (idx % 2) * 4 + 2 * par

        def token_of(idx):
            return ((idx % WPG) // 2) * P

        @block.sync
        def _(sp):
            def natural_rows(dst, src, a):
                sp.dma_start(dst, src.rearrange("(a p) c -> p a c", a=a)).then_inc(w_loaded, 16)

            def load_x(idx, par):
                sp.dma_start(x_tok[:, par, :, :],
                             x[bass.ds(batch_of(idx, par), 2), bass.ds(token_of(idx), P), :].rearrange("b t c -> t b c")
                             ).then_inc(x_loaded[par], 16)

            natural_rows(n_base, W_base, CB)
            for n, w in enumerate((Wq, Wk, Wv)):
                natural_rows(n_qkv[n], w, CB)
            natural_rows(n_o, Wo, CB)
            natural_rows(n_fc, W_fc, FB)
            natural_rows(n_proj, W_proj, CB)
            sp.dma_start(n_As, As.rearrange("e r c -> (e r) c")).then_inc(w_loaded, 16)
            for a in range(CB):
                sp.dma_start(n_Bs[:, a, :].rearrange("p (e r) -> p e r", e=E),
                             Bs[:, a * P:(a + 1) * P, :].rearrange("e o r -> o e r")).then_inc(w_loaded, 16)
            sp.dma_start(n_Wb[0:H, :], Wb).then_inc(w_loaded, 16)
            for n, w in enumerate((conv_q, conv_k, conv_v)):
                sp.dma_start(taps[:, n, :, :], w.rearrange("(a p) k -> p a k", a=CB)).then_inc(c_loaded, 16)
            with nc.allow_non_contiguous_dma(reason="a few vectors as columns"):
                sp.dma_start(bcol[:, :], b_base.rearrange("(a p) -> p a", a=CB)).then_inc(c_loaded, 16)
                sp.dma_start(b2col[:, :], bias2.rearrange("(a p) -> p a", a=CB)).then_inc(c_loaded, 16)
                for h in range(HB):
                    sp.dma_start(normcol[h * D:(h + 1) * D, :],
                                 o_norm_w.rearrange("(d a) -> d a", a=1)).then_inc(c_loaded, 16)
            sp.dma_start(condn[:, :], cond).then_inc(c_loaded, 16)
            for par in range(2):
                load_x(0, par)

            def store_qkv(idx, par, more):
                sp.wait_ge(proj_free, PROJ * (2 * idx + par + 1))
                if more:
                    load_x(idx + 1, par)
                b0, t0 = batch_of(idx, par), token_of(idx)
                for w in range(3):
                    sp.dma_start(qkv_d[w, bass.ds(b0, 2), :, bass.ds(t0, P)].rearrange("b (a p) t -> p (b a) t", a=CB),
                                 act[:, par, w, :, :]).then_inc(qkv_stored[par], 16)
                sp.dma_start(beta_d[bass.ds(b0 * H, 2 * H), bass.ds(t0, P)].rearrange("(b h) t -> h b t", b=2),
                             beta_sb[:, par, :, :]).then_inc(qkv_stored[par], 16)

            def window_load(s):
                group, w, par = s // WPG, s % WPG, s % 2
                for n in range(2):
                    sp.dma_start(
                        kv_w[:, bass.ds(par, 1), n, :, :].rearrange("p o d t -> p (o d) t"),
                        qkv_d[1 + n].rearrange("b (h d) t -> (b h) d t", d=D)[bass.ds(group * P, P), :, bass.ds(w * WIN, WIN)]
                    ).then_inc(win_loaded, 16)
                sp.dma_start(beta_w[:, bass.ds(par, 1), :].rearrange("p o t -> p (o t)"),
                             beta_d[bass.ds(group * P, P), bass.ds(w * WIN, WIN)]).then_inc(win_loaded, 16)

            def unit_loads(idx, par, first):
                if not first:
                    sp.wait_ge(fwd_full, FWD * (idx - 1) + R_MAIN[par] + 2)
                b0, t0 = batch_of(idx, par), token_of(idx)
                row0 = ((idx % 2) * 4 + 2 * par) * H

                def load(dst, src):
                    sp.dma_start(dst, src).then_inc(f_loaded[par], 16)

                load(u_f[:, par, :, :],
                     u_d[bass.ds(b0 * H, 2 * H), :, bass.ds(t0, P)].rearrange("(a h) d t -> (h d) a t", h=HB))
                for dst, n in ((q_f, 0), (k_f, 1)):
                    load(dst[:, par, :, :],
                         qkv_d[n, bass.ds(b0, 2), :, bass.ds(t0, P)].rearrange("b (a p) t -> p (b a) t", a=CB))
                load(s0_f[:, par, :, :],
                     s_d[bass.ds((idx // 2) * 2, 1), bass.ds(row0, 2 * H)].rearrange("o (a h) d m -> (h d) (o a) m", h=HB))
                load(mapb[:, par, :, :], map_d[bass.ds(b0, 2)].rearrange("b (a p) o -> p (b a) o", a=CB))
                load(xf_tok[:, par, :, :],
                     x[bass.ds(b0, 2), bass.ds(t0, P), :].rearrange("b t c -> t b c"))

            for par in range(2):
                store_qkv(0, par, True)
            for g in range(E):
                sp.dma_start(map_w[g * OPG:(g + 1) * OPG, :, :],
                             weight2[g].rearrange("(a o) t -> o a t", o=OPG)).then_inc(map_loaded, 16)
                sp.dma_start(map_m[g * OPG:(g + 1) * OPG, :, :],
                             mask2.rearrange("(a o) t -> o a t", o=OPG)).then_inc(mask_loaded, 16)
            for par in range(2):
                store_qkv(1, par, True)
            for par in range(2):
                sp.wait_ge(qkv_stored[par], 64 * LEAD)
            window_load(0)

            chunk = 0
            for a in range(CB):
                for oq in range(OG // OQ):
                    sp.wait_ge(map_free, OQ * (chunk + 1))
                    sp.dma_start(
                        map_d[:, a * P:(a + 1) * P, oq * OQ * OPG:(oq + 1) * OQ * OPG].rearrange("b t o -> t b o"),
                        map_st[:, chunk % 2, :, :, :].rearrange("t b a o -> t b (a o)")
                    ).then_inc(map_stored[chunk % 2], 16)
                    chunk += 1
            for par in range(2):
                sp.wait_ge(map_stored[par], 16 * (chunk // 2))

            for first, last, flags in SEGMENTS:
                with slots(sp, first, last) as s:
                    if "u" in flags:
                        sp.wait_ge(u_ready, s)
                        group, w = (s - 1) // WPG, (s - 1) % WPG
                        sp.dma_start(u_d[bass.ds(group * P, P), :, bass.ds(w * WIN, WIN)], u_out[:, :, :]
                                     ).then_inc(u_stored, 16)
                    if "w" in flags:
                        sp.wait_ge(dump_ready, s + 1)
                        sp.dma_start(s_d[bass.ds(s, 1)].rearrange("o p k m -> p (o k) m"), dump[:, :, :]
                                     ).then_inc(s_stored, 16)
                    if "f" in flags:
                        sp.wait_ge(u_stored, 16 * s if first <= SLOTS else 16 * SLOTS)
                        sp.sem_inc(sp_turns, 1)
                        sp.wait_ge(s_stored, 16 * (s + 1) if "w" in flags else 16 * SLOTS)
                        for par in range(2):
                            unit_loads(s - FOLLOW, par, first == FOLLOW)
                    if "p" in flags:
                        for par in range(2):
                            store_qkv(s + LEAD, par, "x" in flags)
                    if "n" in flags:
                        if "p" in flags:
                            for par in range(2):
                                sp.wait_ge(qkv_stored[par], 64 * (s + LEAD + 1))
                        if "u" in flags:
                            sp.wait_ge(win_done, s)
                        window_load(s + 1)
                    if "f" in flags:
                        idx = s - FOLLOW
                        for par in range(2):
                            sp.wait_ge(fwd_free, FWD * idx + R_TAIL[par] + 1)
                            sp.dma_start(
                                out[bass.ds(batch_of(idx, par), 2), bass.ds(token_of(idx), P), :].rearrange("b t c -> t b c"),
                                out_sb[:, par, :, :]).then_inc(out_stored[par], 16)
            for par in range(2):
                sp.wait_ge(out_stored[par], 16 * SLOTS)
                sp.wait_ge(qkv_stored[par], 64 * SLOTS)
            sp.wait_ge(u_stored, 16 * SLOTS)
            sp.wait_ge(s_stored, 16 * SLOTS)

        @block.gpsimd
        def _(pool):
            pool.memset(ones, 1.0).then_inc(const_ready, 1)
            pool.wait_ge(const_ready, 1)
            pool.affine_select(out=ident[:, :], in_=ones, compare_op=ALU.is_equal, fill=0.0, base=0,
                               pattern=[[-1, P]], channel_multiplier=1).then_inc(ident_ready, 1)
            pool.memset(carry[:, 0:4, :, :], 0.0).then_inc(pad_ready, 1)
            pool.affine_select(out=half_block.rearrange("p (h m) -> p h m", h=HB),
                               in_=ones.rearrange("p (h m) -> p h m", h=HB), compare_op=ALU.is_ge, fill=0.0,
                               base=0, pattern=[[-D, HB], [0, D]], channel_multiplier=1).then_inc(block_ready, 1)
            pool.wait_ge(block_ready, 1)
            pool.affine_select(out=block_ones[:, :].rearrange("p (h m) -> p h m", h=HB),
                               in_=half_block.rearrange("p (h m) -> p h m", h=HB), compare_op=ALU.is_ge,
                               fill=0.0, base=D - 1, pattern=[[D, HB], [0, D]], channel_multiplier=-1
                               ).then_inc(block_ready, 1)
            pool.wait_ge(block_ready, 2)
            pool.tensor_scalar(block_mean[:, :], block_ones[:, :], 1.0 / D, None, ALU.mult).then_inc(block_ready, 1)

            def carry_tokens(idx, par, first=False):
                n = 2 * idx + par
                place = (idx % WPG) * 2 + par
                if not first:
                    pool.wait_ge(proj_full, PROJ * n)
                    pool.wait_ge(carry_saved, n)
                    pool.wait_ge(head_ready, n)
                    pool.sem_inc(pool_turns, 1)
                pool.tensor_copy(pre[:, :, 0:TAPS - 1],
                                 carry[:, bass.ds(place, 1), :, :].rearrange("p o a k -> p (o a) k")
                                 ).then_inc(head_ready, 1)
                pool.wait_ge(proj_free, PROJ * n + 6)
                pool.sem_inc(pool_turns, 1)
                pool.tensor_copy(carry[:, bass.ds(place + 4, 1), :, :].rearrange("p o a k -> p (o a) k"),
                                 pre[:, :, P:P + TAPS - 1]).then_inc(carry_saved, 1)

            pool.wait_ge(pad_ready, 1)
            for idx in range(LEAD):
                for par in range(2):
                    carry_tokens(idx, par, first=(idx + par == 0))
                if idx == 0:
                    pool.wait_ge(map_loaded, 16 * E)
                    pool.wait_ge(mask_loaded, 16 * E)
                    pool.tensor_tensor(map_w, map_w, map_m, ALU.mult).then_inc(map_masked, 1)
            pool.wait_ge(map_full, CB * OG)
            pool.memset(u_pad, 0.0).then_inc(pad_ready, 1)
            edges = spike_thresholds()

            def attend(idx, par, first):
                n = 2 * idx + par
                at = ATT * n
                pool.wait_ge(f_loaded[par], 16 * F_DMAS * (idx + 1))
                if not (first and par == 0):
                    pool.wait_ge(fwd_full, FWD * idx + (R_O[0] + 1 if par else 1 + R_O[1] - FWD))
                for bc in range(BC):
                    last = pool.tensor_tensor(
                        s0_block[:, bc, :, :],
                        s0_f[:, par, bc, :].rearrange("p (u m) -> p u m", u=1).broadcast_to([P, HB, D]),
                        block_ones[:, :].rearrange("p (h m) -> p h m", h=HB), ALU.mult)
                last.then_inc(s0_ready, 1)
                pool.wait_ge(att_free, at + 1)
                pool.sem_inc(pool_turns, 1)
                pool.tensor_scalar(guard[:, :], guard[:, :], L2_EPS * L2_EPS, RMS_EPS * D, ALU.max, ALU.mult
                                   ).then_inc(guard_ready, 1)
                for j in range(GRAMS):
                    pool.wait_ge(att_free, at + 2 + j)
                    pool.sem_inc(pool_turns, 1)
                    pool.affine_select(out=pm[:, j % 2, :, :], in_=pm[:, j % 2, :, :], compare_op=ALU.is_ge, fill=0.0,
                                       base=0, pattern=[[0, 4], [1, P]], channel_multiplier=-1).then_inc(pm_ready, 1)
                pool.wait_ge(att_free, at + ATT)
                pool.wait_ge(guard_ready, n + 1)
                pool.tensor_tensor(scale_f[:, par, :], scale_f[:, par, :], guard[:, :], ALU.add).then_inc(square_ready, 1)

            def scale_o(idx, par):
                pool.wait_ge(norm_inverse, 2 * idx + par + 1)
                o = o_f[:, par, :, :, :].rearrange("p b a t -> p (b a t)")
                pool.tensor_tensor(o, o, scale_f[:, par, :], ALU.mult).then_inc(o_ready, 1)

            def squares(idx, par):
                for k in range(FB // 2):
                    pool.wait_ge(fwd_free, FWD * idx + R_MAIN[par] + 3 + k)
                    h = hid[:, 2 * k:2 * k + 2, :, :]
                    pool.tensor_tensor(h, h, h, ALU.mult).then_inc(hid_squared, 1)

            def spikes(idx, par):
                done = NUM_STEPS * (2 * idx + par)
                pool.wait_ge(fwd_free, FWD * idx + R_MAIN[par] + 7)
                pool.sem_inc(pool_turns, 1)
                pool.tensor_scalar(count[:, :], drive[:, par, :], edges[0], None, ALU.is_gt).then_inc(count_done, 1)
                compared = (NUM_STEPS - 1) * (2 * idx + par)
                for n in range(1, NUM_STEPS):
                    pool.tensor_scalar(over[:, :], drive[:, par, :], edges[n], None, ALU.is_gt).then_inc(over_ready, 1)
                    pool.wait_ge(over_ready, compared + n)
                    if n == 1:
                        pool.wait_ge(count_done, done + 1)
                    pool.tensor_tensor(count[:, :], count[:, :], over[:, :], ALU.add).then_inc(count_done, 1)
                    pool.wait_ge(count_done, done + n + 1)
                    pool.sem_inc(pool_turns, 1)
                pool.tensor_scalar(count[:, :], count[:, :], 1.0 / NUM_STEPS, None, ALU.mult).then_inc(rate_ready, 1)
                pool.wait_ge(rate_ready, 2 * idx + par + 1)
                pool.tensor_tensor(total[:, par, :, :, :].rearrange("p b a t -> p (b a t)"), count[:, :],
                                   x2T[:, par, :, :, :].rearrange("p b a t -> p (b a t)"), ALU.add
                                   ).then_inc(total_ready, 1)

            for first, last, flags in SEGMENTS:
                with slots(pool, first, last) as s:
                    if "p" in flags:
                        for par in range(2):
                            carry_tokens(s + LEAD, par)
                    if "f" in flags:
                        idx = s - FOLLOW
                        for par in range(2):
                            attend(idx, par, first == FOLLOW)
                        scale_o(idx, 0)
                        squares(idx, 0)
                        scale_o(idx, 1)
                        spikes(idx, 0)
                        squares(idx, 1)
                        spikes(idx, 1)

        @block.vector
        def _(dve):
            seq = [0]

            def then(ins):
                seq[0] += 1
                ins.then_inc(dve_seq, 1)
                dve.wait_ge(dve_seq, seq[0])

            dve.wait_ge(ident_ready, 1)
            then(dve.tensor_reduce(pick[:, :], ident[:, :].rearrange("p (g o) -> p o g", g=E), AX_X, ALU.add))
            dve.wait_ge(c_loaded, 16 * (6 + HB))
            dve.tensor_copy(cond_wide[:, :, :], condn[:, :].rearrange("b (e u) -> b e u", u=1).broadcast_to([B, E, RANK])
                            ).then_inc(wide_ready, 1)
            for n in range(3):
                for a in range(CB):
                    for k in range(TAPS):
                        dve.tensor_scalar(diag[:, n, a, k, :], ident[:, :], taps[:, n, a, k:k + 1], None,
                                          ALU.mult).then_inc(diag_ready, 1)
            dve.wait_ge(setup_free, JOBS)
            dve.tensor_tensor(pick_cond[:, :, :], pick[:, :].rearrange("p (o u) -> p o u", u=1).broadcast_to([P, OPG, B]),
                              cond_rows[:, :].rearrange("p (u b) -> p u b", u=1).broadcast_to([P, OPG, B]),
                              ALU.mult).then_inc(pick_ready, 1)

            base = seq[0]
            CHAIN = 2 + 8

            def links(part):
                at = [0]

                def go(ins):
                    at[0] += 1
                    ins.then_inc(dve_seq, 1)
                    dve.wait_ge(dve_seq, part + at[0])
                return go

            def norm_sum(go, s, par):
                dve.wait_ge(win_loaded, 48 * (s + 1))
                k = kv_w[:, par, 0, :, :]
                go(dve.tensor_tensor(sqr, k, k, ALU.mult))
                go(dve.tensor_reduce(ss[:, :], sqr.rearrange("p d t -> p t d"), AX_X, ALU.add))
                dve.tensor_scalar(ss[:, :], ss[:, :], L2_EPS * L2_EPS, None, ALU.max).then_inc(ss_ready, 1)

            def norm_invert(go, s, par):
                dve.wait_ge(root_ready, s + 1)
                r = rinv[:, par, :]
                go(dve.reciprocal(r, root[:, :]))
                go(dve.tensor_tensor(tmp[:, :], r, r, ALU.mult))
                go(dve.tensor_tensor(tmp[:, :], tmp[:, :], ss[:, :], ALU.mult))
                go(dve.tensor_scalar(tmp[:, :], tmp[:, :], -0.5, 1.5, ALU.mult, ALU.add))
                go(dve.tensor_tensor(r, r, tmp[:, :], ALU.mult))
                go(dve.tensor_tensor(rk_beta[:, par, :], r, beta_w[:, par, :], ALU.mult))
                k = kv_w[:, par, 0, :, :]
                go(dve.tensor_tensor(kb[:, :, :], k, rk_beta[:, par, :].rearrange("p (u t) -> p u t", u=1).broadcast_to(
                    [P, D, WIN]), ALU.mult))
                go(dve.tensor_tensor(k, k, r.rearrange("p (u t) -> p u t", u=1).broadcast_to([P, D, WIN]), ALU.mult))

            def invert_o_norm(idx, par):
                dve.wait_ge(norm_root, 2 * idx + par + 1)
                dve.reciprocal(scale_f[:, par, :], scale_f[:, par, :]).then_inc(norm_inverse, 1)

            def over_rows(v):
                return v.rearrange("p d u -> p u d").broadcast_to([P, DM, D])

            def steps(par, first, last):
                kn, v = kv_w[:, par, 0], kv_w[:, par, 1]
                half = [slice(h * DM, (h + 1) * DM) for h in range(MH)]
                for t in range(first, last):
                    one, at = slice(t, t + 1), MH * t
                    prod = prod_ring[:, t % RING, :, :]
                    if t % RING == 0:
                        dve.tensor_scalar(prod_ring[:, :, :, D:D + 1].rearrange("p r m u -> p r (m u)"),
                                          v[:, :, t:t + RING].rearrange("p m r -> p r m"), -1.0, None, ALU.mult
                                          ).then_inc(v_placed, 1)
                    for h in range(MH):
                        if t:
                            dve.wait_ge(state_done, at - MH + h + 1)
                        dve.tensor_tensor(prod[:, half[h], 0:D], state[:, half[h], :], over_rows(kn[:, :, one]), ALU.mult
                                          ).then_inc(kprod_done, 1)
                    if t % RING == 0:
                        dve.wait_ge(v_placed, t // RING + 1)
                    for h in range(MH):
                        dve.wait_ge(kprod_done, at + h + 1)
                        dve.tensor_reduce(w_all[:, half[h], one].rearrange("p m u -> p (m u)"), prod[:, half[h], :],
                                          AX_X, ALU.add).then_inc(w_done, 1)
                    for h in range(MH):
                        dve.wait_ge(w_done, at + h + 1)
                        dve.tensor_tensor(outer[:, half[h], :], w_all[:, half[h], one].broadcast_to([P, DM, D]),
                                          over_rows(kb[:, :, one]), ALU.mult).then_inc(outer_done, 1)
                    for h in range(MH):
                        dve.wait_ge(outer_done, at + h + 1)
                        dve.tensor_tensor(state[:, half[h], :], state[:, half[h], :], outer[:, half[h], :],
                                          ALU.subtract).then_inc(state_done, 1)

            def window(s, w, group, flags):
                par = w % 2
                go = links(base + CHAIN + s * CHAIN)
                if "u" in flags:
                    dve.wait_ge(state_done, MH * WIN)
                if w == 0:
                    dve.memset(state[:, :, :], 0.0).then_inc(state_clear, 1)
                    dve.wait_ge(state_clear, group + 1)
                if "u" in flags:
                    dve.wait_ge(s_stored, 16 * s)
                dve.tensor_copy(dump[:, :, :], state[:, :, :].rearrange("p m k -> p k m")).then_inc(dump_ready, 1)
                if "u" in flags:
                    for counter in (v_placed, kprod_done, w_done, outer_done, state_done):
                        dve.sem_clear(counter)
                steps(par, 0, WIN // 2)
                if "n" in flags:
                    norm_sum(go, s + 1, 1 - par)
                steps(par, WIN // 2, 3 * WIN // 4)
                if "f" in flags:
                    for unit in range(2):
                        invert_o_norm(s - FOLLOW, unit)
                steps(par, 3 * WIN // 4, WIN)
                dve.wait_ge(w_done, MH * WIN)
                if "u" in flags:
                    dve.wait_ge(u_stored, 16 * s)
                dve.scalar_tensor_tensor(out=u_out[:, :, :], in0=w_all[:, :, :], scalar=-1.0,
                                         in1=rk_beta[:, par, :].rearrange("p (u t) -> p u t", u=1).broadcast_to([P, D, WIN]),
                                         op0=ALU.mult, op1=ALU.mult).then_inc(u_ready, 1)
                if "n" in flags:
                    norm_invert(go, s + 1, 1 - par)
                dve.wait_ge(u_ready, s + 1)
                dve.sem_inc(win_done, 1)

            go = links(base)
            norm_sum(go, 0, 0)
            norm_invert(go, 0, 0)
            window(0, 0, 0, "n")
            window(1, 1, 0, "nu")
            with dve.Fori(0, GROUPS - 1) as i:
                for w in range(FOLLOW, FOLLOW + WPG):
                    window(WPG * i + w, w % WPG, i + w // WPG, "nuf")
            window(SLOTS - 2, WPG - 2, GROUPS - 1, "nuf")
            window(SLOTS - 1, WPG - 1, GROUPS - 1, "uf")
            for idx in range(SLOTS - FOLLOW, SLOTS):
                for par in range(2):
                    invert_o_norm(idx, par)

        @block.scalar
        def _(act_e):
            act_e.wait_ge(c_loaded, 16 * (6 + HB))
            for j, (blocks, dest, kind) in enumerate(jobs):
                act_e.wait_ge(setup_full, j + 1)
                width = sum(b.shape[0] for b in blocks)
                src = proj_ps[:, j % 4, 0:width]
                if len(dest.shape) == 3:
                    src = src.rearrange("p (a e) -> p a e", a=dest.shape[1])
                scale = {"copy": 1.0, "norm": normcol[:, 0:1], "scaling": ALPHA / RANK}[kind]
                act_e.activation(dest, src, ACT.Copy, scale=scale).then_inc(setup_free, 1)
            act_e.wait_ge(setup_full, JOBS)
            rows = proj_ps[:, (JOBS - 1) % 4, 0:B]
            for h in range(2):
                act_e.activation(cond_units[:, :, h, :], rows.rearrange("p (g b) -> p g b", g=GROUPS), ACT.Copy)
            act_e.activation(cond_rows[:, :], rows, ACT.Copy).then_inc(setup_free, 1)

            def project(idx, par, first=False):
                n = 2 * idx + par
                ring = [(PROJ * par + k) % 4 for k in range(PROJ)]

                def full(k):
                    act_e.wait_ge(proj_full, PROJ * n + k + 1)

                def bank(k):
                    return proj_ps[:, ring[k], :].rearrange("p (b a t) -> p b a t", b=2, a=CB)

                full(0)
                act_e.activation(xT[:, :, :, :], bank(0), ACT.Copy).then_inc(proj_free, 1)
                full(1)
                units = cond_units[:, :, :, :].rearrange("p g h b -> p (g h b)")
                for b in range(2):
                    last = act_e.activation(loraT[:, b, :], proj_ps[:, ring[1], b * P:(b + 1) * P], ACT.Copy,
                                            scale=units[:, bass.ds(2 * n + b, 1)])
                last.then_inc(proj_free, 1)
                full(2)
                for a in range(CB):
                    last = act_e.activation(yT[:, :, a, :], bank(2)[:, :, a, :], ACT.Identity, bias=bcol[:, a:a + 1])
                last.then_inc(proj_free, 1)
                if not (first and par == 0):
                    act_e.wait_ge(carry_saved, n)
                for w in range(3):
                    full(3 + w)
                    act_e.activation(pre[:, w * BC:(w + 1) * BC, TAPS - 1:],
                                     proj_ps[:, ring[3 + w], :].rearrange("p (a t) -> p a t", a=BC), ACT.Copy
                                     ).then_inc(proj_free, 1)
                if not first:
                    act_e.wait_ge(qkv_stored[par], 64 * idx)
                full(6)
                act_e.activation(beta_sb[:, par, :, :],
                                 proj_ps[0:H, ring[6], 0:2 * P].rearrange("p (b t) -> p b t", b=2), ACT.Sigmoid
                                 ).then_inc(proj_free, 1)
                for w in range(3):
                    full(7 + w)
                    act_e.activation(act[:, par, w, :, :], proj_ps[:, ring[7 + w], :].rearrange("p (a t) -> p a t", a=BC),
                                     ACT.Silu).then_inc(proj_free, 1)

            def fwd_bank(r):
                return fwd_ps[:, r % 2, :]

            def attend(idx, par):
                n = 2 * idx + par
                act_e.wait_ge(f_loaded[par], 16 * F_DMAS * (idx + 1))
                act_e.activation(qsq, q_f[:, par, :, :].rearrange("p a t -> p (a t)"), ACT.Square).then_inc(qsq_ready, 1)

                def masked_q(j):
                    for i in range(4):
                        h = (j % 2) * 4 + i
                        last = act_e.activation(qm[:, j % 2, i, :], q_f[:, par, j // 2, :], ACT.Copy,
                                                scale=block_ones[:, h * D:h * D + 1])
                    last.then_inc(qm_ready, 1)

                masked_q(0)
                masked_q(1)
                act_e.wait_ge(fwd_full, FWD * idx + R_U[par] + 1)
                act_e.activation(u_pad.rearrange("p a (h x) -> p a h x", x=PAD)[:, :, :, 0:D],
                                 fwd_bank(R_U[par]).rearrange("p (a h m) -> p a h m", a=BC, h=HB), ACT.Copy
                                 ).then_inc(fwd_free, 1)
                act_e.wait_ge(att_full, ATT * n + 1)
                act_e.activation(guard[:, :], fwd_ps[:, 2, :], ACT.Copy).then_inc(att_free, 1)
                for j in range(GRAMS):
                    act_e.wait_ge(att_full, ATT * n + j + 2)
                    act_e.activation(pm[:, j % 2, :, :], fwd_ps[:, 2 + (1 + j) % 2, :].rearrange("p (h t) -> p h t", h=4),
                                     ACT.Copy).then_inc(att_free, 1)
                    if j + 2 < GRAMS:
                        masked_q(j + 2)
                act_e.wait_ge(fwd_full, FWD * idx + R_O[par] + 1)
                act_e.activation(osq[:, :], fwd_bank(R_O[par]), ACT.Square)
                act_e.activation(o_f[:, par, :, :, :].rearrange("p b a t -> p (b a t)"), fwd_bank(R_O[par]), ACT.Copy
                                 ).then_inc(fwd_free, 1)
                act_e.wait_ge(att_full, ATT * (n + 1))
                act_e.activation(scale_f[:, par, :], fwd_ps[:, 2 + (ATT - 1) % 2, :], ACT.Copy).then_inc(att_free, 1)
                act_e.wait_ge(square_ready, n + 1)
                act_e.activation(scale_f[:, par, :], scale_f[:, par, :], ACT.Sqrt).then_inc(norm_root, 1)

            def forward_main(idx, par):
                def full(k):
                    act_e.wait_ge(fwd_full, FWD * idx + R_MAIN[par] + k + 1)

                def bank(k):
                    return fwd_bank(R_MAIN[par] + k)

                full(0)
                act_e.activation(x2T[:, par, :, :, :].rearrange("p b a t -> p (b a t)"), bank(0), ACT.Copy
                                 ).then_inc(fwd_free, 1)
                full(1)
                for a in range(CB):
                    last = act_e.activation(zT[:, :, a, :], bank(1).rearrange("p (b a t) -> p b a t", b=2, a=CB)[:, :, a, :],
                                            ACT.Identity, bias=b2col[:, a:a + 1])
                last.then_inc(fwd_free, 1)
                for k in range(FB // 2):
                    full(2 + k)
                    act_e.activation(hid[:, 2 * k:2 * k + 2, :, :].rearrange("p f b t -> p (f b t)"), bank(2 + k), ACT.Relu
                                     ).then_inc(fwd_free, 1)
                full(6)
                act_e.activation(drive[:, par, :], bank(6), ACT.Copy).then_inc(fwd_free, 1)

            def forward_tail(idx, par, first):
                act_e.wait_ge(fwd_full, FWD * idx + R_TAIL[par] + 1)
                if not first:
                    act_e.wait_ge(out_stored[par], 16 * idx)
                act_e.activation(out_sb[:, par, :, :].rearrange("p b c -> p (b c)"), fwd_bank(R_TAIL[par]), ACT.Copy
                                 ).then_inc(fwd_free, 1)

            def root_next(s):
                act_e.wait_ge(ss_ready, s + 1)
                act_e.activation(root[:, :], ss[:, :], ACT.Sqrt).then_inc(root_ready, 1)

            act_e.wait_ge(setup_free, JOBS)
            for idx in range(LEAD):
                for par in range(2):
                    project(idx, par, first=(idx == 0))
            root_next(0)

            use, chunk = 0, 0
            for a in range(CB):
                for oq in range(OG // OQ):
                    if chunk >= 2:
                        act_e.wait_ge(map_stored[chunk % 2], 16 * (chunk // 2))
                    for k in range(OQ):
                        act_e.wait_ge(map_full, use + 1)
                        act_e.activation(map_st[:, chunk % 2, :, k, :],
                                         fwd_ps[:, use % 4, :].rearrange("p (o b) -> p b o", o=OPG), ACT.Copy
                                         ).then_inc(map_free, 1)
                        use += 1
                    chunk += 1
            act_e.wait_ge(pad_ready, 2)
            act_e.wait_ge(block_ready, 3)

            for first, last, flags in SEGMENTS:
                with slots(act_e, first, last) as s:
                    if "p" in flags:
                        for par in range(2):
                            project(s + LEAD, par)
                    if "f" in flags:
                        for par in range(2):
                            attend(s - FOLLOW, par)
                    if "n" in flags:
                        root_next(s + 1)
                    if "f" in flags:
                        for par in range(2):
                            forward_main(s - FOLLOW, par)
                        for par in range(2):
                            forward_tail(s - FOLLOW, par, first == FOLLOW)

        @block.tensor
        def _(pe):
            pe.wait_ge(ident_ready, 1)
            pe.wait_ge(w_loaded, 16 * 11)
            for j, (blocks, dest, kind) in enumerate(jobs):
                if j >= 4:
                    pe.wait_ge(setup_free, j - 3)
                at = 0
                for b in blocks:
                    rows = b.shape[0]
                    last = pe.transpose(proj_ps[:, j % 4, at:at + rows], b, ident[0:rows, 0:rows])
                    at += rows
                last.then_inc(setup_full, 1)
            pe.wait_ge(setup_free, JOBS - 4)
            pe.wait_ge(wide_ready, 1)
            pe.matmul(proj_ps[:, (JOBS - 1) % 4, 0:B], cond_wide[:, :, :].rearrange("b e r -> b (e r)"),
                      ident[0:B, 0:B], start=True, stop=True).then_inc(setup_full, 1)
            pe.wait_ge(setup_free, JOBS)
            pe.wait_ge(diag_ready, 3 * CB * TAPS)

            def project(idx, par, first=False):
                n = 2 * idx + par
                ring = [(PROJ * par + k) % 4 for k in range(PROJ)]

                def free(k):
                    if not (first and PROJ * par + k < 4):
                        pe.wait_ge(proj_free, PROJ * n + k - 3)

                def read(k):
                    pe.wait_ge(proj_free, PROJ * n + k + 1)

                def bank(k):
                    return proj_ps[:, ring[k], :].rearrange("p (b a t) -> p b a t", b=2, a=CB)

                pe.wait_ge(x_loaded[par], 16 * (idx + 1))
                free(0)
                for b in range(2):
                    for a in range(CB):
                        last = pe.transpose(bank(0)[:, b, a, :], x_tok[:, par, b, a * P:(a + 1) * P], ident[:, :])
                last.then_inc(proj_full, 1)
                free(1)
                read(0)
                for c in range(CB):
                    last = pe.matmul(proj_ps[:, ring[1], 0:2 * P], AsT[:, c, :], xT[:, :, c, :],
                                     start=(c == 0), stop=(c == CB - 1))
                last.then_inc(proj_full, 1)
                free(2)
                for a in range(CB):
                    for c in range(CB):
                        pe.matmul(bank(2)[:, :, a, :], WbaseT[:, c, a * P:(a + 1) * P], xT[:, :, c, :],
                                  start=(c == 0), stop=False)
                    if a == 0:
                        read(1)
                    last = pe.matmul(bank(2)[:, :, a, :], BsT[:, a * P:(a + 1) * P], loraT[:, :, :], start=False, stop=True)
                last.then_inc(proj_full, 1)
                read(2)
                for w in range(3):
                    free(3 + w)
                    for a in range(CB):
                        for c in range(CB):
                            last = pe.matmul(bank(3 + w)[:, :, a, :], WqkvT[:, w, c, a * P:(a + 1) * P], yT[:, :, c, :],
                                             start=(c == 0), stop=(c == CB - 1))
                    last.then_inc(proj_full, 1)
                free(6)
                for c in range(CB):
                    last = pe.matmul(proj_ps[0:H, ring[6], 0:2 * P], WbT[:, c, :], yT[:, :, c, :],
                                     start=(c == 0), stop=(c == CB - 1))
                last.then_inc(proj_full, 1)
                for w in range(3):
                    free(7 + w)
                    read(3 + w)
                    if w == 0:
                        pe.wait_ge(head_ready, n + 1)
                    for a in range(CB):
                        for k in range(TAPS):
                            last = pe.matmul(bank(7 + w)[:, :, a, :], diag[:, w, a, k, :],
                                             pre[:, w * BC:(w + 1) * BC, k:k + P].rearrange(
                                                 "p (b a) t -> p b a t", a=CB)[:, :, a, :],
                                             start=(k == 0), stop=(k == TAPS - 1))
                    last.then_inc(proj_full, 1)

            def fwd_bank(r):
                return fwd_ps[:, r % 2, :].rearrange("p (b a t) -> p b a t", b=2, a=CB)

            def fwd_turn(idx, r, first):
                if not (first and r < 2):
                    pe.wait_ge(fwd_free, FWD * idx + r - 1)

            def attend(idx, par, first):
                n = 2 * idx + par
                at = ATT * n

                def att_turn(i):
                    if not (first and par == 0 and i < 2):
                        pe.wait_ge(att_free, at + i - 1)

                pe.wait_ge(f_loaded[par], 16 * F_DMAS * (idx + 1))
                fwd_turn(idx, R_U[par], first)
                for bc in range(BC):
                    last = pe.transpose(fwd_ps[:, R_U[par] % 2, bc * P:(bc + 1) * P], u_f[:, par, bc, :], ident[:, :])
                last.then_inc(fwd_full, 1)
                att_turn(0)
                pe.wait_ge(qsq_ready, n + 1)
                pe.matmul(fwd_ps[:, 2, :], block_ones[:, :], qsq, start=True, stop=True).then_inc(att_full, 1)

                def gram(j):
                    att_turn(1 + j)
                    pe.wait_ge(qm_ready, GRAMS * n + j + 1)
                    pe.matmul(fwd_ps[:, 2 + (1 + j) % 2, :], k_f[:, par, j // 2, :], qm[:, j % 2, :, :],
                              start=True, stop=True).then_inc(att_full, 1)

                def answer(j):
                    bc, hh = j // 2, j % 2
                    o = fwd_ps[:, R_O[par] % 2, bc * P:(bc + 1) * P]
                    pe.wait_ge(pm_ready, GRAMS * n + j + 1)
                    for i in range(4):
                        h = hh * 4 + i
                        pe.matmul(o, u_pad[:, bc, h * P:(h + 1) * P], pm[:, j % 2, i, :], start=(h == 0), stop=False)
                    if hh == 1:
                        return pe.matmul(o, s0_block[:, bc, :, :].rearrange("p h m -> p (h m)"), q_f[:, par, bc, :],
                                         start=False, stop=True)

                gram(0)
                gram(1)
                pe.wait_ge(fwd_free, FWD * idx + R_U[par] + 1)
                pe.wait_ge(s0_ready, n + 1)
                for j in range(GRAMS):
                    last = answer(j)
                    if j + 2 < GRAMS:
                        gram(j + 2)
                last.then_inc(fwd_full, 1)
                att_turn(ATT - 1)
                pe.wait_ge(fwd_free, FWD * idx + R_O[par] + 1)
                pe.matmul(fwd_ps[:, 2 + (ATT - 1) % 2, :], block_mean[:, :], osq[:, :], start=True, stop=True
                          ).then_inc(att_full, 1)

            def forward_main(idx, par):
                n = 2 * idx + par

                def turn(k):
                    fwd_turn(idx, R_MAIN[par] + k, False)

                def read(k):
                    pe.wait_ge(fwd_free, FWD * idx + R_MAIN[par] + k + 1)

                def bank(k):
                    return fwd_bank(R_MAIN[par] + k)

                turn(0)
                pe.wait_ge(o_ready, n + 1)
                for a in range(CB):
                    for c in range(CB):
                        pe.matmul(bank(0)[:, :, a, :], WoT[:, c, a * P:(a + 1) * P], o_f[:, par, :, c, :],
                                  start=(c == 0), stop=False, skip_group_check=True)
                    for b in range(2):
                        last = pe.matmul(bank(0)[:, b, a, :], xf_tok[:, par, b, a * P:(a + 1) * P], ident[:, :],
                                         start=False, stop=True, skip_group_check=True)
                last.then_inc(fwd_full, 1)
                turn(1)
                read(0)
                for b in range(2):
                    for a in range(CB):
                        for c in range(CB):
                            last = pe.matmul(bank(1)[:, b, a, :], mapb[:, par, b * CB + c, a * P:(a + 1) * P],
                                             x2T[:, par, b, c, :], start=(c == 0), stop=(c == CB - 1))
                last.then_inc(fwd_full, 1)
                read(1)
                for k in range(FB // 2):
                    turn(2 + k)
                    for a in range(2):
                        f = 2 * k + a
                        for c in range(CB):
                            last = pe.matmul(fwd_ps[:, (R_MAIN[par] + 2 + k) % 2, a * 2 * P:(a + 1) * 2 * P],
                                             WfcT[:, c, f * P:(f + 1) * P], zT[:, :, c, :],
                                             start=(c == 0), stop=(c == CB - 1))
                    last.then_inc(fwd_full, 1)
                turn(6)
                for a in range(CB):
                    for f in range(FB):
                        if a == 0 and f % 2 == 0:
                            pe.wait_ge(hid_squared, (FB // 2) * n + f // 2 + 1)
                        last = pe.matmul(bank(6)[:, :, a, :], WprojT[:, f, a * P:(a + 1) * P], hid[:, f, :, :],
                                         start=(f == 0), stop=(f == FB - 1))
                last.then_inc(fwd_full, 1)

            def forward_tail(idx, par):
                fwd_turn(idx, R_TAIL[par], False)
                pe.wait_ge(total_ready, 2 * idx + par + 1)
                for b in range(2):
                    for a in range(CB):
                        last = pe.transpose(fwd_bank(R_TAIL[par])[:, b, a, :], total[:, par, b, a, :], ident[:, :])
                last.then_inc(fwd_full, 1)

            for idx in range(LEAD):
                for par in range(2):
                    project(idx, par, first=(idx == 0))

            pe.wait_ge(map_masked, 1)
            pe.wait_ge(pick_ready, 1)
            use = 0
            for a in range(CB):
                for og in range(OG):
                    if use >= 4:
                        pe.wait_ge(map_free, use - 3)
                    pe.matmul(fwd_ps[:, use % 4, :], map_w[:, og, a * P:(a + 1) * P], pick_cond[:, :, :],
                              start=True, stop=True).then_inc(map_full, 1)
                    use += 1
            pe.wait_ge(map_free, use)
            pe.wait_ge(block_ready, 3)

            for first, last_, flags in SEGMENTS:
                with slots(pe, first, last_) as s:
                    if "p" in flags:
                        for par in range(2):
                            project(s + LEAD, par)
                    if "f" in flags:
                        for par in range(2):
                            attend(s - FOLLOW, par, first == FOLLOW)
                        for par in range(2):
                            forward_main(s - FOLLOW, par)
                        for par in range(2):
                            forward_tail(s - FOLLOW, par)


INS = ['x', 'cond_8', 'L0_cond_W_base', 'L0_cond_b_base', 'L0_cond_As', 'L0_cond_Bs', 'L0_attn_Wq', 'L0_attn_Wk',
       'L0_attn_Wv', 'L0_attn_Wb', 'L0_attn_Wo', 'L0_attn_conv_q', 'L0_attn_conv_k', 'L0_attn_conv_v',
       'L0_attn_o_norm_w', 'L0_cond2_weight', 'L0_cond2_mask', 'L0_cond2_bias', 'L0_ffn_W_fc', 'L0_ffn_W_proj']


def kernel(**inputs):
    import numpy as _np
    import concourse.bacc as _bacc
    from concourse import mybir as _mybir
    from concourse.bass_utils import run_bass_kernel_spmd as _run

    nc = _bacc.Bacc("TRN2", target_bir_lowering=False, num_devices=1)
    arrays, args = {}, []
    for name in INS:
        a = _np.ascontiguousarray(inputs[name])
        arrays[f"in_{name}"] = a
        args.append(nc.dram_tensor(f"in_{name}", a.shape, _mybir.dt.from_np(a.dtype), kind="ExternalInput").ap())
    out = nc.dram_tensor("out", inputs["x"].shape, _mybir.dt.float32, kind="ExternalOutput").ap()
    adaln_attention_ffn(nc, *args, out)
    r = _run(nc, [arrays], core_ids=[0])
    return r.results[0]["out"]
```

```python
from contextlib import ExitStack, contextmanager

import numpy as np

import concourse.bass as bass
from concourse import mybir

F32 = mybir.dt.float32
ALU = mybir.AluOpType
ACT = mybir.ActivationFunctionType
AX_X = mybir.AxisListType.X
P = 128

ALPHA, RANK = 32.0, 16
L2_EPS, RMS_EPS = 1e-6, 1e-6
BETA, THRESHOLD, NUM_STEPS = 0.9, 1.0, 5


def spike_thresholds():
    f = np.float32

    def count(y):
        mem, spikes = f(0), 0
        for _ in range(NUM_STEPS):
            reset = f(mem - f(THRESHOLD) > 0)
            mem = f(f(f(BETA) * mem) + y) - reset * f(THRESHOLD)
            spikes += int(mem - f(THRESHOLD) > 0)
        return spikes

    edges = []
    for n in range(1, NUM_STEPS + 1):
        low, high = int(f(0.125).view(np.uint32)), int(f(8.0).view(np.uint32))
        while high - low > 1:
            mid = (low + high) // 2
            if count(np.uint32(mid).view(np.float32)) >= n:
                high = mid
            else:
                low = mid
        edges.append(float(np.uint32(low).view(np.float32)))
    return edges


def adaln_attention_ffn(nc, x, cond, W_base, b_base, As, Bs, Wq, Wk, Wv, Wb, Wo, conv_q, conv_k,
                        conv_v, o_norm_w, weight2, mask2, bias2, W_fc, W_proj, out):
    B, T, C = x.shape
    H = Wb.shape[0]
    D = C // H
    E = cond.shape[1]
    F = W_fc.shape[0]
    TAPS = conv_q.shape[1]
    CB = C // P
    FB = F // P
    HB = P // D
    GB = P // H
    GROUPS = B // GB
    WIN = 64
    WPG = T // WIN
    SLOTS = GROUPS * WPG
    BC = 2 * CB
    UPG = 2 * WPG
    RING = 8
    INVERT = (36, 52)
    MH = 2
    DM = D // MH
    LEAD, FOLLOW = 3, 2
    OPG = P // E
    OG = C // OPG
    OQ = 4
    assert T == 2 * P and D * H == C and E * RANK == P and WIN % (4 * RING) == 0

    SEGMENTS = [(0, 1, "pxw"), (1, FOLLOW, "pxwnu"), (FOLLOW, FOLLOW + 1, "pxfwnu"),
                (FOLLOW + 1, FOLLOW + 2, "pxftwnu"), (FOLLOW + 2, SLOTS - LEAD - 1, "pxftwnu"),
                (SLOTS - LEAD - 1, SLOTS - LEAD, "pftwnu"), (SLOTS - LEAD, SLOTS - 1, "ftwnu"),
                (SLOTS - 1, SLOTS, "ftwu"), (SLOTS, SLOTS + 1, "ftu"), (SLOTS + 1, SLOTS + FOLLOW, "ft"),
                (SLOTS + FOLLOW, SLOTS + FOLLOW + 1, "t")]
    FIRST_F, FIRST_T = FOLLOW, FOLLOW + 1

    @contextmanager
    def slots(eng, first, last):
        if last - first == 1:
            yield first
        else:
            with eng.Fori(first, last) as s:
                yield s

    qkv_d = nc.dram_tensor("qkv_scratch", [3, B, C, T], F32).ap()
    beta_d = nc.dram_tensor("beta_scratch", [B * H, T], F32).ap()
    u_d = nc.dram_tensor("u_scratch", [B * H, D, T], F32).ap()
    s_d = nc.dram_tensor("state_scratch", [SLOTS, P, D, D], F32).ap()
    map_d = nc.dram_tensor("map_scratch", [B, C, C], F32).ap()

    with ExitStack() as ctx:
        def sb(name, shape):
            return ctx.enter_context(nc.sbuf_tensor(name, shape, F32))

        def sem(name):
            return ctx.enter_context(nc.semaphore(name))

        ident = sb("ident", [P, P])
        block_ones = sb("block_ones", [P, P])
        block_mean = sb("block_mean", [P, P])
        WbaseT = sb("WbaseT", [P, CB, C])
        WqkvT = sb("WqkvT", [P, 3, CB, C])
        WoT = sb("WoT", [P, CB, C])
        WbT = sb("WbT", [P, CB, H])
        AsT = sb("AsT", [P, CB, P])
        BsT = sb("BsT", [P, C])
        WfcT = sb("WfcT", [P, CB, F])
        WprojT = sb("WprojT", [P, FB, C])
        taps = sb("taps", [P, 3, CB, TAPS])
        diag = sb("diag", [P, 3, CB, TAPS, P])
        bcol = sb("bcol", [P, CB])
        b2col = sb("b2col", [P, CB])
        normcol = sb("normcol", [P, 1])
        condn = sb("condn", [B, E])
        cond_rows = sb("cond_rows", [P, B])
        cond_units = sb("cond_units", [P, GROUPS, 2, GB])
        pick = sb("pick", [P, OPG])

        region = sb("region", [P, 8192])
        region_2 = sb("region_2", [P, 4096])

        def carve(tensor):
            at = [0]

            def take(n):
                at[0] += n
                return tensor[:, at[0] - n:at[0]]
            return take

        nat = carve(region)
        n_base = nat(CB * C).rearrange("p (a c) -> p a c", a=CB)
        n_qkv = [nat(CB * C).rearrange("p (a c) -> p a c", a=CB) for _ in range(3)]
        n_o = nat(CB * C).rearrange("p (a c) -> p a c", a=CB)
        n_As = nat(C)
        n_Bs = nat(CB * P).rearrange("p (a e) -> p a e", a=CB)
        n_Wb = nat(C)
        n_fc = nat(FB * C).rearrange("p (a c) -> p a c", a=FB)
        n_proj = nat(CB * F).rearrange("p (a f) -> p a f", a=CB)
        map_w = region[:, 0:OG * C].rearrange("p (a t) -> p a t", a=OG)
        map_m = region[:, OG * C:2 * OG * C].rearrange("p (a t) -> p a t", a=OG)
        map_st = region_2[:, :].rearrange("p (i b k o) -> p i b k o", i=2, b=B, k=OQ)
        late = carve(region)
        PAD = P + D
        u_pad = late(BC * HB * PAD).rearrange("p (a x) -> p a x", a=BC)
        hid = late(FB * 2 * P).rearrange("p (f b t) -> p f b t", f=FB, b=2)
        x2T = late(2 * BC * P).rearrange("p (i b a t) -> p i b a t", i=2, b=2, a=CB)
        qsq = late(BC * P)
        late_2 = carve(region_2)
        qm = late_2(2 * 4 * P).rearrange("p (i h t) -> p i h t", i=2, h=4)
        pm = late_2(2 * 4 * P).rearrange("p (i h t) -> p i h t", i=2, h=4)
        drive = late_2(2 * BC * P).rearrange("p (i x) -> p i x", i=2)
        total = late_2(2 * BC * P).rearrange("p (i b a t) -> p i b a t", i=2, b=2, a=CB)

        x_tok = sb("x_tok", [P, 2, 2, C])
        xT = sb("xT", [P, 2, CB, P])
        loraT = sb("loraT", [P, 2, P])
        yT = sb("yT", [P, 2, CB, P])
        pre = sb("pre", [P, 3 * BC, TAPS - 1 + P])
        carry = sb("carry", [P, UPG + 4, 3 * BC, TAPS - 1])
        act = sb("act", [P, 2, 3, BC, P])
        beta_sb = sb("beta_sb", [H, 2, 2, P])
        kv_w = sb("kv_w", [P, 2, 2, D, WIN])
        beta_w = sb("beta_w", [P, 2, WIN])
        w_all = sb("w_all", [P, D, WIN])
        u_out = sb("u_out", [P, D, WIN])
        state = sb("state", [P, D, D])
        dump = sb("dump", [P, D, D])
        prod_ring = sb("prod_ring", [P, RING, D, D + 1])
        ksq = sb("ksq", [P, D, WIN])
        outer = sb("outer", [P, D, D])
        ss = sb("ss", [P, WIN])
        root = sb("root", [P, WIN])
        rinv = sb("rinv", [P, WIN])
        key_scale = sb("key_scale", [P, 2, WIN])
        xf_tok = sb("xf_tok", [P, 2, 2, C])
        q_f = sb("q_f", [P, 2, BC, P])
        k_f = sb("k_f", [P, 2, BC, P])
        u_f = sb("u_f", [P, 2, BC, P])
        s0_f = sb("s0_f", [P, 2, BC, D])
        mapb = sb("mapb", [P, 2, BC, C])
        s0_block = sb("s0_block", [P, BC, HB, D])
        least = sb("least", [P, 2])
        osq = sb("osq", [P, BC * P])
        over = osq
        ones, half_block = osq[:, 0:P], osq[:, P:2 * P]
        cond_wide = osq[0:B, 2 * P:3 * P].rearrange("b (e r) -> b e r", e=E)
        guard = sb("guard", [P, BC * P])
        count = guard
        pick_cond = guard[:, :].rearrange("p (o b) -> p o b", o=OPG)
        o_f = sb("o_f", [P, 2, 2, CB, P])
        scale_f = sb("scale_f", [P, 2, BC * P])
        zT = sb("zT", [P, 2, CB, P])
        out_sb = sb("out_sb", [P, 2, 2, C])

        banks = ctx.enter_context(nc.psum_tensor("banks", [P, 8, 512], F32))

        w_loaded, c_loaded, map_loaded, mask_loaded = map(sem, ("w_loaded", "c_loaded", "map_loaded", "mask_loaded"))
        const_ready, ident_ready = sem("const_ready"), sem("ident_ready")
        block_ready = sem("block_ready")
        pm_ready, square_ready = sem("pm_ready"), sem("square_ready")
        setup_full, setup_free = sem("setup_full"), sem("setup_free")
        late_loaded, late_full, late_free = sem("late_loaded"), sem("late_full"), sem("late_free")
        map_full, map_free = sem("map_full"), sem("map_free")
        map_masked, pick_ready = sem("map_masked"), sem("pick_ready")
        map_stored = [sem("map_stored0"), sem("map_stored1")]
        diag_ready, wide_ready, pad_ready = sem("diag_ready"), sem("wide_ready"), sem("pad_ready")
        x_loaded = [sem("x_loaded0"), sem("x_loaded1")]
        proj_full, proj_free = sem("proj_full"), sem("proj_free")
        head_ready, carry_saved = sem("head_ready"), sem("carry_saved")
        qkv_stored = [sem("qkv_stored0"), sem("qkv_stored1")]
        win_loaded, second_loaded, win_done = sem("win_loaded"), sem("second_loaded"), sem("win_done")
        ss_ready, root_ready = sem("ss_ready"), sem("root_ready")
        u_ready, u_stored = sem("u_ready"), sem("u_stored")
        dump_ready, s_stored = sem("dump_ready"), sem("s_stored")
        v_placed, kprod_done, w_done, outer_done, state_done = map(
            sem, ("v_placed", "kprod_done", "w_done", "outer_done", "state_done"))
        ksq_ready, scale_ready, key_ready = sem("ksq_ready"), sem("scale_ready"), sem("key_ready")
        dve_seq, state_clear = sem("dve_seq"), sem("state_clear")
        pool_turns, sp_turns, act_turns = map(sem, ("pool_turns", "sp_turns", "act_turns"))
        f_loaded = [sem("f_loaded0"), sem("f_loaded1")]
        fwd_full, fwd_free = sem("fwd_full"), sem("fwd_free")
        att_full, att_free = sem("att_full"), sem("att_free")
        s0_ready, qsq_ready, qm_ready = sem("s0_ready"), sem("qsq_ready"), sem("qm_ready")
        norm_root, norm_inverse, o_ready = sem("norm_root"), sem("norm_inverse"), sem("o_ready")
        hid_squared, over_ready, rate_ready = sem("hid_squared"), sem("over_ready"), sem("rate_ready")
        count_done = [sem("count_done0"), sem("count_done1")]
        total_ready = [sem("total_ready0"), sem("total_ready1")]
        out_stored = [sem("out_stored0"), sem("out_stored1")]

        PROJ = 10
        GRAMS = BC * HB // 4
        ATT = GRAMS + 2
        RESULTS = ["u0", "o0", "u1", "x0", "z0", "o1", "f00", "f01", "f02", "f03", "y0",
                   "x1", "z1", "f10", "f11", "f12", "f13", "y1", "t0", "t1"]
        FWD = len(RESULTS)
        AT = {name: r for r, name in enumerate(RESULTS)}
        ringed = [name for name in RESULTS if name[0] != "o"]
        assert len(ringed) % 3 == 0 and PROJ % 2 == 0 and ATT % 2 == 0
        BANK = {name: 2 + i % 3 for i, name in enumerate(ringed)} | {"o0": 5, "o1": 5}

        def before(name):
            seen = [r for r in range(-FWD, AT[name]) if BANK[RESULTS[r % FWD]] == BANK[name]]
            return seen[-1]

        MAIN = [["x0", "z0", "f00", "f01", "f02", "f03", "y0"], ["x1", "z1", "f10", "f11", "f12", "f13", "y1"]]
        F_DMAS = 6

        edges = spike_thresholds()
        block = ctx.enter_context(nc.Block())

        jobs = []

        def job(blocks, dest, kind="copy"):
            jobs.append((blocks, dest, kind))

        job([n_As[:, a * P:(a + 1) * P] for a in range(CB)], AsT[:, :, :])
        job([n_Bs[:, a, :] for a in range(CB)], BsT[:, :], "scaling")
        for a in range(CB):
            job([n_Wb[0:H, a * P:(a + 1) * P]], WbT[:, a, :])
        for a in range(CB):
            job([n_base[:, o, a * P:(a + 1) * P] for o in range(CB)], WbaseT[:, a, :])
            for n in range(3):
                job([n_qkv[n][:, o, a * P:(a + 1) * P] for o in range(CB)], WqkvT[:, n, a, :])
        JOBS = len(jobs) + 1
        for a in range(CB):
            job([n_o[:, o, a * P:(a + 1) * P] for o in range(CB)], WoT[:, a, :], "norm")
            for h in range(FB // 4):
                job([n_fc[:, 4 * h + o, a * P:(a + 1) * P] for o in range(4)],
                    WfcT[:, a, h * 512:(h + 1) * 512])
        for f in range(FB):
            job([n_proj[:, o, f * P:(f + 1) * P] for o in range(CB)], WprojT[:, f, :])
        jobs, late_jobs = jobs[:JOBS - 1], jobs[JOBS - 1:]

        def batch_of(idx, par):
            return (idx // WPG) * GB + (idx % 2) * 4 + 2 * par

        def window_here(s):
            if isinstance(s, int) and s < 2:
                return (win_loaded, second_loaded)[s], 48
            return win_loaded, 48 * s

        def token_of(idx):
            return ((idx % WPG) // 2) * P

        @block.sync
        def _(sp):
            def natural_rows(dst, src, a, loaded):
                sp.dma_start(dst, src.rearrange("(a p) c -> p a c", a=a)).then_inc(loaded, 16)

            def load_x(idx, par):
                sp.dma_start(x_tok[:, par, :, :],
                             x[bass.ds(batch_of(idx, par), 2), bass.ds(token_of(idx), P), :].rearrange("b t c -> t b c")
                             ).then_inc(x_loaded[par], 16)

            sp.dma_start(n_As, As.rearrange("e r c -> (e r) c")).then_inc(w_loaded, 16)
            for a in range(CB):
                sp.dma_start(n_Bs[:, a, :].rearrange("p (e r) -> p e r", e=E),
                             Bs[:, a * P:(a + 1) * P, :].rearrange("e o r -> o e r")).then_inc(w_loaded, 16)
            sp.dma_start(n_Wb[0:H, :], Wb).then_inc(w_loaded, 16)
            natural_rows(n_base, W_base, CB, w_loaded)
            for n, w in enumerate((Wq, Wk, Wv)):
                natural_rows(n_qkv[n], w, CB, w_loaded)
            for par in range(2):
                load_x(0, par)
            sp.dma_start(condn[:, :], cond).then_inc(c_loaded, 16)
            for n, w in enumerate((conv_q, conv_k, conv_v)):
                sp.dma_start(taps[:, n, :, :], w.rearrange("(a p) k -> p a k", a=CB)).then_inc(c_loaded, 16)
            with nc.allow_non_contiguous_dma(reason="a few vectors as columns"):
                sp.dma_start(bcol[:, :], b_base.rearrange("(a p) -> p a", a=CB)).then_inc(c_loaded, 16)
                sp.dma_start(b2col[:, :], bias2.rearrange("(a p) -> p a", a=CB)).then_inc(c_loaded, 16)
                for h in range(HB):
                    sp.dma_start(normcol[h * D:(h + 1) * D, :],
                                 o_norm_w.rearrange("(d a) -> d a", a=1)).then_inc(c_loaded, 16)
            natural_rows(n_o, Wo, CB, late_loaded)
            natural_rows(n_fc, W_fc, FB, late_loaded)
            natural_rows(n_proj, W_proj, CB, late_loaded)

            def store_qkv(idx, par, more):
                sp.wait_ge(proj_free, PROJ * (2 * idx + par + 1))
                if more:
                    load_x(idx + 1, par)
                b0, t0 = batch_of(idx, par), token_of(idx)
                for w in range(3):
                    sp.dma_start(qkv_d[w, bass.ds(b0, 2), :, bass.ds(t0, P)].rearrange("b (a p) t -> p (b a) t", a=CB),
                                 act[:, par, w, :, :]).then_inc(qkv_stored[par], 16)
                sp.dma_start(beta_d[bass.ds(b0 * H, 2 * H), bass.ds(t0, P)].rearrange("(b h) t -> h b t", b=2),
                             beta_sb[:, par, :, :]).then_inc(qkv_stored[par], 16)

            def window_load(s, loaded):
                group, w, par = s // WPG, s % WPG, s % 2
                for n in range(2):
                    sp.dma_start(
                        kv_w[:, bass.ds(par, 1), n, :, :].rearrange("p o d t -> p (o d) t"),
                        qkv_d[1 + n].rearrange("b (h d) t -> (b h) d t", d=D)[bass.ds(group * P, P), :, bass.ds(w * WIN, WIN)]
                    ).then_inc(loaded, 16)
                sp.dma_start(beta_w[:, bass.ds(par, 1), :].rearrange("p o t -> p (o t)"),
                             beta_d[bass.ds(group * P, P), bass.ds(w * WIN, WIN)]).then_inc(loaded, 16)

            def unit_loads(idx, par, first):
                if not first:
                    sp.wait_ge(fwd_full, FWD * (idx - 1) + AT[f"z{par}"] + 1)
                b0, t0 = batch_of(idx, par), token_of(idx)
                row0 = ((idx % 2) * 4 + 2 * par) * H

                def load(dst, src):
                    sp.dma_start(dst, src).then_inc(f_loaded[par], 16)

                load(u_f[:, par, :, :],
                     u_d[bass.ds(b0 * H, 2 * H), :, bass.ds(t0, P)].rearrange("(a h) d t -> (h d) a t", h=HB))
                for dst, n in ((q_f, 0), (k_f, 1)):
                    load(dst[:, par, :, :],
                         qkv_d[n, bass.ds(b0, 2), :, bass.ds(t0, P)].rearrange("b (a p) t -> p (b a) t", a=CB))
                load(s0_f[:, par, :, :],
                     s_d[bass.ds((idx // 2) * 2, 1), bass.ds(row0, 2 * H)].rearrange("o (a h) d m -> (h d) (o a) m", h=HB))
                load(mapb[:, par, :, :], map_d[bass.ds(b0, 2)].rearrange("b (a p) o -> p (b a) o", a=CB))
                load(xf_tok[:, par, :, :],
                     x[bass.ds(b0, 2), bass.ds(t0, P), :].rearrange("b t c -> t b c"))

            for idx in range(2):
                for par in range(2):
                    store_qkv(idx, par, True)
            for par in range(2):
                sp.wait_ge(qkv_stored[par], 64 * 2)
            window_load(0, win_loaded)
            window_load(1, second_loaded)
            sp.wait_ge(late_full, len(late_jobs))
            for g in range(E):
                sp.dma_start(map_w[g * OPG:(g + 1) * OPG, :, :],
                             weight2[g].rearrange("(a o) t -> o a t", o=OPG)).then_inc(map_loaded, 16)
                sp.dma_start(map_m[g * OPG:(g + 1) * OPG, :, :],
                             mask2.rearrange("(a o) t -> o a t", o=OPG)).then_inc(mask_loaded, 16)
            for par in range(2):
                store_qkv(2, par, True)

            chunk = 0
            for a in range(CB):
                for oq in range(OG // OQ):
                    sp.wait_ge(map_free, OQ * (chunk + 1))
                    sp.dma_start(
                        map_d[:, a * P:(a + 1) * P, oq * OQ * OPG:(oq + 1) * OQ * OPG].rearrange("b t o -> t b o"),
                        map_st[:, chunk % 2, :, :, :].rearrange("t b a o -> t b (a o)")
                    ).then_inc(map_stored[chunk % 2], 16)
                    chunk += 1
            for par in range(2):
                sp.wait_ge(map_stored[par], 16 * (chunk // 2))

            for first, last, flags in SEGMENTS:
                with slots(sp, first, last) as s:
                    if "u" in flags:
                        sp.wait_ge(u_ready, s)
                        group, w = (s - 1) // WPG, (s - 1) % WPG
                        sp.dma_start(u_d[bass.ds(group * P, P), :, bass.ds(w * WIN, WIN)], u_out[:, :, :]
                                     ).then_inc(u_stored, 16)
                    if "n" in flags:
                        for par in range(2):
                            sp.wait_ge(qkv_stored[par], 64 * (s + LEAD) if "p" in flags else 64 * SLOTS)
                        if "u" in flags:
                            sp.wait_ge(win_done, s)
                        window_load(s + 1, win_loaded)
                    if "w" in flags:
                        sp.wait_ge(dump_ready, s + 1)
                        sp.dma_start(s_d[bass.ds(s, 1)].rearrange("o p k m -> p (o k) m"), dump[:, :, :]
                                     ).then_inc(s_stored, 16)
                    if "f" in flags:
                        sp.wait_ge(u_stored, 16 * s if first <= SLOTS else 16 * SLOTS)
                        sp.sem_inc(sp_turns, 1)
                        sp.wait_ge(s_stored, 16 * (s + 1) if "w" in flags else 16 * SLOTS)
                        for par in range(2):
                            unit_loads(s - FOLLOW, par, first == FOLLOW)
                    if "p" in flags:
                        store_qkv(s + LEAD, 0, "x" in flags)
                    if "t" in flags:
                        idx = s - FOLLOW - 1
                        for par in range(2):
                            sp.wait_ge(fwd_free, FWD * idx + AT[f"t{par}"] + 1)
                            sp.dma_start(
                                out[bass.ds(batch_of(idx, par), 2), bass.ds(token_of(idx), P), :].rearrange("b t c -> t b c"),
                                out_sb[:, par, :, :]).then_inc(out_stored[par], 16)
                    if "p" in flags:
                        store_qkv(s + LEAD, 1, "x" in flags)
            for par in range(2):
                sp.wait_ge(out_stored[par], 16 * SLOTS)
                sp.wait_ge(qkv_stored[par], 64 * SLOTS)
            sp.wait_ge(u_stored, 16 * SLOTS)
            sp.wait_ge(s_stored, 16 * SLOTS)

        @block.gpsimd
        def _(pool):
            pool.memset(ones, 1.0).then_inc(const_ready, 1)
            pool.wait_ge(const_ready, 1)
            pool.affine_select(out=ident[:, :], in_=ones, compare_op=ALU.is_equal, fill=0.0, base=0,
                               pattern=[[-1, P]], channel_multiplier=1).then_inc(ident_ready, 1)
            for i, sign in enumerate((-1.0, 1.0)):
                pool.memset(least[:, i:i + 1], sign * RMS_EPS * D * L2_EPS * L2_EPS).then_inc(const_ready, 1)
            pool.memset(carry[:, 0:4, :, :], 0.0).then_inc(pad_ready, 1)
            pool.affine_select(out=half_block.rearrange("p (h m) -> p h m", h=HB),
                               in_=ones.rearrange("p (h m) -> p h m", h=HB), compare_op=ALU.is_ge, fill=0.0,
                               base=0, pattern=[[-D, HB], [0, D]], channel_multiplier=1).then_inc(block_ready, 1)
            pool.wait_ge(block_ready, 1)
            pool.affine_select(out=block_ones[:, :].rearrange("p (h m) -> p h m", h=HB),
                               in_=half_block.rearrange("p (h m) -> p h m", h=HB), compare_op=ALU.is_ge,
                               fill=0.0, base=D - 1, pattern=[[D, HB], [0, D]], channel_multiplier=-1
                               ).then_inc(block_ready, 1)
            pool.wait_ge(block_ready, 2)
            pool.tensor_scalar(block_mean[:, :], block_ones[:, :], 1.0 / D, None, ALU.mult).then_inc(block_ready, 1)

            def place(idx, par):
                return (idx % WPG) * 2 + par

            def carry_in(idx, par, first=False):
                n = 2 * idx + par
                if not first:
                    pool.wait_ge(proj_full, PROJ * n)
                    pool.wait_ge(carry_saved, n)
                    pool.wait_ge(head_ready, n)
                    pool.sem_inc(pool_turns, 1)
                pool.tensor_copy(pre[:, :, 0:TAPS - 1],
                                 carry[:, bass.ds(place(idx, par), 1), :, :].rearrange("p o a k -> p (o a) k")
                                 ).then_inc(head_ready, 1)

            def carry_out(idx, par):
                pool.wait_ge(proj_free, PROJ * (2 * idx + par) + 6)
                pool.sem_inc(pool_turns, 1)
                pool.tensor_copy(carry[:, bass.ds(place(idx, par) + 4, 1), :, :].rearrange("p o a k -> p (o a) k"),
                                 pre[:, :, P:P + TAPS - 1]).then_inc(carry_saved, 1)

            def key_squares(s):
                pool.wait_ge(*window_here(s))
                pool.sem_inc(pool_turns, 1)
                k = kv_w[:, bass.ds(s % 2, 1), 0, :, :].rearrange("p o d t -> p (o d) t")
                pool.tensor_tensor(ksq[:, :, :], k, k, ALU.mult).then_inc(ksq_ready, 1)

            def scale_keys(s):
                pool.wait_ge(scale_ready, s + 1)
                pool.sem_inc(pool_turns, 1)
                k = kv_w[:, bass.ds(s % 2, 1), 0, :, :].rearrange("p o d t -> p (o d) t")
                pool.tensor_tensor(k, k, key_scale[:, bass.ds(s % 2, 1), :].broadcast_to([P, D, WIN]), ALU.mult
                                   ).then_inc(key_ready, 1)

            pool.wait_ge(pad_ready, 1)
            for idx in range(LEAD):
                for par in range(2):
                    carry_in(idx, par, first=(idx + par == 0))
                    carry_out(idx, par)
                if idx == 1:
                    key_squares(0)
                    scale_keys(0)
                    key_squares(1)
            pool.wait_ge(map_loaded, 16 * E)
            pool.wait_ge(mask_loaded, 16 * E)
            pool.tensor_tensor(map_w, map_w, map_m, ALU.mult).then_inc(map_masked, 1)
            scale_keys(1)
            pool.wait_ge(map_full, CB * OG)
            pool.memset(u_pad, 0.0).then_inc(pad_ready, 1)
            carry_in(LEAD, 0)

            def start_state(idx, par, first):
                pool.wait_ge(f_loaded[par], 16 * F_DMAS * (idx + 1))
                if not (first and par == 0):
                    pool.wait_ge(fwd_full, FWD * idx + AT["o0"] + 1 if par else FWD * (idx - 1) + AT["o1"] + 1)
                for bc in range(BC):
                    last = pool.tensor_tensor(
                        s0_block[:, bc, :, :],
                        s0_f[:, par, bc, :].rearrange("p (u m) -> p u m", u=1).broadcast_to([P, HB, D]),
                        block_ones[:, :].rearrange("p (h m) -> p h m", h=HB), ALU.mult)
                last.then_inc(s0_ready, 1)

            def mask_grams(idx, par, grams):
                for j in grams:
                    pool.wait_ge(att_free, ATT * (2 * idx + par) + 2 + j)
                    pool.sem_inc(pool_turns, 1)
                    pool.affine_select(out=pm[:, j % 2, :, :], in_=pm[:, j % 2, :, :], compare_op=ALU.is_ge, fill=0.0,
                                       base=0, pattern=[[0, 4], [1, P]], channel_multiplier=-1).then_inc(pm_ready, 1)

            def add_guard(idx, par):
                n = 2 * idx + par
                pool.wait_ge(att_free, ATT * (n + 1))
                pool.tensor_tensor(scale_f[:, par, :], scale_f[:, par, :], guard[:, :], ALU.add).then_inc(square_ready, 1)

            def scale_o(idx, par):
                pool.wait_ge(norm_inverse, 2 * idx + par + 1)
                o = o_f[:, par, :, :, :].rearrange("p b a t -> p (b a t)")
                pool.tensor_tensor(o, o, scale_f[:, par, :], ALU.mult).then_inc(o_ready, 1)

            def squares(idx, par):
                for k in range(FB // 2):
                    pool.wait_ge(fwd_free, FWD * idx + AT[f"f{par}{k}"] + 1)
                    h = hid[:, 2 * k:2 * k + 2, :, :]
                    pool.tensor_tensor(h, h, h, ALU.mult).then_inc(hid_squared, 1)

            def spikes(idx):
                done, compared = NUM_STEPS * idx, (NUM_STEPS - 1) * idx
                pool.wait_ge(fwd_free, FWD * idx + AT["y0"] + 1)
                pool.sem_inc(pool_turns, 1)
                pool.tensor_scalar(count[:, :], drive[:, 0, :], edges[0], None, ALU.is_gt).then_inc(count_done[0], 1)
                for n in range(1, NUM_STEPS):
                    pool.tensor_scalar(over[:, :], drive[:, 0, :], edges[n], None, ALU.is_gt).then_inc(over_ready, 1)
                    pool.wait_ge(over_ready, compared + n)
                    if n == 1:
                        pool.wait_ge(count_done[0], done + 1)
                    pool.tensor_tensor(count[:, :], count[:, :], over[:, :], ALU.add).then_inc(count_done[0], 1)
                    pool.wait_ge(count_done[0], done + n + 1)
                    pool.sem_inc(pool_turns, 1)
                pool.tensor_scalar(count[:, :], count[:, :], 1.0 / NUM_STEPS, None, ALU.mult).then_inc(rate_ready, 1)
                pool.wait_ge(rate_ready, idx + 1)
                pool.tensor_tensor(total[:, 0, :, :, :].rearrange("p b a t -> p (b a t)"), count[:, :],
                                   x2T[:, 0, :, :, :].rearrange("p b a t -> p (b a t)"), ALU.add
                                   ).then_inc(total_ready[0], 1)

            for first, last, flags in SEGMENTS:
                with slots(pool, first, last) as s:
                    nxt, idx = s + LEAD, s - FOLLOW
                    if "n" in flags:
                        key_squares(s + 1)
                    if "p" in flags:
                        carry_out(nxt, 0)
                    if "f" in flags:
                        start_state(idx, 0, first == FIRST_F)
                    if "p" in flags:
                        carry_in(nxt, 1)
                    if "f" in flags:
                        mask_grams(idx, 0, range(6))
                    if "p" in flags:
                        carry_out(nxt, 1)
                    if "f" in flags:
                        mask_grams(idx, 0, range(6, GRAMS))
                        add_guard(idx, 0)
                        start_state(idx, 1, False)
                        mask_grams(idx, 1, range(4))
                        scale_o(idx, 0)
                        mask_grams(idx, 1, range(4, GRAMS))
                        add_guard(idx, 1)
                        squares(idx, 0)
                        scale_o(idx, 1)
                    if "n" in flags:
                        scale_keys(s + 1)
                    if "f" in flags:
                        squares(idx, 1)
                    if "x" in flags:
                        carry_in(nxt + 1, 0)
                    if "f" in flags:
                        spikes(idx)

        @block.vector
        def _(dve):
            seq = [0]

            def then(ins):
                seq[0] += 1
                ins.then_inc(dve_seq, 1)
                dve.wait_ge(dve_seq, seq[0])

            dve.wait_ge(ident_ready, 1)
            then(dve.tensor_reduce(pick[:, :], ident[:, :].rearrange("p (g o) -> p o g", g=E), AX_X, ALU.add))
            dve.wait_ge(c_loaded, 16 * (6 + HB))
            dve.tensor_copy(cond_wide[:, :, :], condn[:, :].rearrange("b (e u) -> b e u", u=1).broadcast_to([B, E, RANK])
                            ).then_inc(wide_ready, 1)
            for n in range(3):
                for a in range(CB):
                    for k in range(TAPS):
                        dve.tensor_scalar(diag[:, n, a, k, :], ident[:, :], taps[:, n, a, k:k + 1], None,
                                          ALU.mult).then_inc(diag_ready, 1)
            dve.wait_ge(setup_free, JOBS)
            dve.tensor_tensor(pick_cond[:, :, :], pick[:, :].rearrange("p (o u) -> p o u", u=1).broadcast_to([P, OPG, B]),
                              cond_rows[:, :].rearrange("p (u b) -> p u b", u=1).broadcast_to([P, OPG, B]),
                              ALU.mult).then_inc(pick_ready, 1)

            base = seq[0]
            CHAIN = 1 + 1

            def links(part):
                at = [0]

                def go(ins):
                    at[0] += 1
                    ins.then_inc(dve_seq, 1)
                    dve.wait_ge(dve_seq, part + at[0])
                return go

            def norm_sum(go, s):
                dve.wait_ge(ksq_ready, s + 1)
                go(dve.tensor_reduce(ss[:, :], ksq[:, :, :].rearrange("p d t -> p t d"), AX_X, ALU.add))
                dve.tensor_scalar(ss[:, :], ss[:, :], L2_EPS * L2_EPS, None, ALU.max).then_inc(ss_ready, 1)

            def norm_invert(go, s, par):
                dve.wait_ge(root_ready, s + 1)
                r = rinv[:, :]
                go(dve.reciprocal(r, root[:, :]))
                dve.tensor_tensor(key_scale[:, par, :], r, beta_w[:, par, :], ALU.mult).then_inc(scale_ready, 1)

            def invert_o_norm(idx, par):
                dve.wait_ge(norm_root, 2 * idx + par + 1)
                dve.reciprocal(scale_f[:, par, :], scale_f[:, par, :]).then_inc(norm_inverse, 1)

            def spikes(idx):
                sum_ = total[:, 1, :, :, :].rearrange("p b a t -> p (b a t)")
                done = NUM_STEPS * idx
                dve.wait_ge(fwd_free, FWD * idx + AT["y1"] + 1)
                dve.tensor_scalar(sum_, drive[:, 1, :], edges[0], None, ALU.is_gt).then_inc(count_done[1], 1)
                for n in range(1, NUM_STEPS):
                    dve.wait_ge(count_done[1], done + n)
                    dve.scalar_tensor_tensor(out=sum_, in0=drive[:, 1, :], scalar=edges[n], in1=sum_,
                                             op0=ALU.is_gt, op1=ALU.add).then_inc(count_done[1], 1)
                dve.wait_ge(count_done[1], done + NUM_STEPS)
                dve.scalar_tensor_tensor(out=sum_, in0=sum_, scalar=1.0 / NUM_STEPS,
                                         in1=x2T[:, 1, :, :, :].rearrange("p b a t -> p (b a t)"),
                                         op0=ALU.mult, op1=ALU.add).then_inc(total_ready[1], 1)

            def over_rows(v):
                return v.rearrange("p d u -> p u d").broadcast_to([P, DM, D])

            def steps(par, first, last):
                kappa, v = kv_w[:, par, 0], kv_w[:, par, 1]
                half = [slice(h * DM, (h + 1) * DM) for h in range(MH)]
                for t in range(first, last):
                    one, at = slice(t, t + 1), MH * t
                    prod = prod_ring[:, t % RING, :, :]
                    if t % RING == 0:
                        dve.scalar_tensor_tensor(
                            out=prod_ring[:, :, :, D:D + 1].rearrange("p r m u -> p r (m u)"),
                            in0=v[:, :, t:t + RING].rearrange("p m r -> p r m"), scalar=-1.0,
                            in1=beta_w[:, par, t:t + RING].rearrange("p (r u) -> p r u", u=1).broadcast_to([P, RING, D]),
                            op0=ALU.mult, op1=ALU.mult).then_inc(v_placed, 1)
                    for h in range(MH):
                        if t:
                            dve.wait_ge(state_done, at - MH + h + 1)
                        dve.tensor_tensor(prod[:, half[h], 0:D], state[:, half[h], :], over_rows(kappa[:, :, one]), ALU.mult
                                          ).then_inc(kprod_done, 1)
                    if t % RING == 0:
                        dve.wait_ge(v_placed, t // RING + 1)
                    for h in range(MH):
                        dve.wait_ge(kprod_done, at + h + 1)
                        dve.tensor_reduce(w_all[:, half[h], one].rearrange("p m u -> p (m u)"), prod[:, half[h], :],
                                          AX_X, ALU.add).then_inc(w_done, 1)
                    for h in range(MH):
                        dve.wait_ge(w_done, at + h + 1)
                        dve.tensor_tensor(outer[:, half[h], :], w_all[:, half[h], one].broadcast_to([P, DM, D]),
                                          over_rows(kappa[:, :, one]), ALU.mult).then_inc(outer_done, 1)
                    for h in range(MH):
                        dve.wait_ge(outer_done, at + h + 1)
                        dve.tensor_tensor(state[:, half[h], :], state[:, half[h], :], outer[:, half[h], :],
                                          ALU.subtract).then_inc(state_done, 1)

            def window(s, w, group, flags):
                par = w % 2
                go = links(base + CHAIN + s * CHAIN)
                if "u" in flags:
                    dve.wait_ge(state_done, MH * WIN)
                if w == 0:
                    dve.memset(state[:, :, :], 0.0).then_inc(state_clear, 1)
                    dve.wait_ge(state_clear, group + 1)
                if "u" in flags:
                    dve.wait_ge(s_stored, 16 * s)
                dve.tensor_copy(dump[:, :, :], state[:, :, :].rearrange("p m k -> p k m")).then_inc(dump_ready, 1)
                if "u" in flags:
                    for counter in (v_placed, kprod_done, w_done, outer_done, state_done):
                        dve.sem_clear(counter)
                if "t" in flags:
                    spikes(s - FOLLOW - 1)
                dve.wait_ge(key_ready, s + 1)
                steps(par, 0, WIN // 4)
                if "n" in flags:
                    norm_sum(go, s + 1)
                steps(par, WIN // 4, INVERT[0])
                if "f" in flags:
                    invert_o_norm(s - FOLLOW, 0)
                steps(par, INVERT[0], INVERT[1])
                if "f" in flags:
                    invert_o_norm(s - FOLLOW, 1)
                if "n" in flags:
                    norm_invert(go, s + 1, 1 - par)
                steps(par, INVERT[1], WIN)
                dve.wait_ge(w_done, MH * WIN)
                if "u" in flags:
                    dve.wait_ge(u_stored, 16 * s)
                dve.scalar_tensor_tensor(out=u_out[:, :, :], in0=w_all[:, :, :], scalar=-1.0,
                                         in1=key_scale[:, par, :].rearrange("p (u t) -> p u t", u=1).broadcast_to([P, D, WIN]),
                                         op0=ALU.mult, op1=ALU.mult).then_inc(u_ready, 1)
                dve.wait_ge(u_ready, s + 1)
                dve.sem_inc(win_done, 1)

            go = links(base)
            norm_sum(go, 0)
            norm_invert(go, 0, 0)
            window(0, 0, 0, "n")
            window(1, 1, 0, "nu")
            window(2, 2, 0, "nuf")
            with dve.Fori(0, GROUPS - 1) as i:
                for w in range(FIRST_T, FIRST_T + WPG):
                    window(WPG * i + w, w % WPG, i + w // WPG, "nuft")
            window(SLOTS - 1, WPG - 1, GROUPS - 1, "uft")
            for idx in range(SLOTS - FOLLOW, SLOTS):
                spikes(idx - 1)
                for par in range(2):
                    invert_o_norm(idx, par)
            spikes(SLOTS - 1)

        @block.scalar
        def _(act_e):
            def transposed(j, job_, bank, full, free):
                blocks, dest, kind = job_
                act_e.wait_ge(full, j + 1)
                src = banks[:, bank, 0:sum(b.shape[0] for b in blocks)]
                if len(dest.shape) == 3:
                    src = src.rearrange("p (a e) -> p a e", a=dest.shape[1])
                scale = {"copy": 1.0, "norm": normcol[:, 0:1], "scaling": ALPHA / RANK}[kind]
                act_e.activation(dest, src, ACT.Copy, scale=scale).then_inc(free, 1)

            for j, job_ in enumerate(jobs):
                transposed(j, job_, j % 4, setup_full, setup_free)
            act_e.wait_ge(setup_full, JOBS)
            rows = banks[:, (JOBS - 1) % 4, 0:B]
            for h in range(2):
                act_e.activation(cond_units[:, :, h, :], rows.rearrange("p (g b) -> p g b", g=GROUPS), ACT.Copy)
            act_e.activation(cond_rows[:, :], rows, ACT.Copy).then_inc(setup_free, 1)

            def project(idx, par, parts=range(PROJ), first=False):
                n = 2 * idx + par
                ring = [k % 2 for k in range(PROJ)]

                def full(k):
                    act_e.wait_ge(proj_full, PROJ * n + k + 1)

                def bank(k):
                    return banks[:, ring[k], :].rearrange("p (b a t) -> p b a t", b=2, a=CB)

                if 0 in parts:
                    full(0)
                    act_e.activation(xT[:, :, :, :], bank(0), ACT.Copy).then_inc(proj_free, 1)
                if 1 in parts:
                    full(1)
                    units = cond_units[:, :, :, :].rearrange("p g h b -> p (g h b)")
                    for b in range(2):
                        last = act_e.activation(loraT[:, b, :], banks[:, ring[1], b * P:(b + 1) * P], ACT.Copy,
                                                scale=units[:, bass.ds(2 * n + b, 1)])
                    last.then_inc(proj_free, 1)
                if 2 in parts:
                    full(2)
                    for a in range(CB):
                        last = act_e.activation(yT[:, :, a, :], bank(2)[:, :, a, :], ACT.Identity, bias=bcol[:, a:a + 1])
                    last.then_inc(proj_free, 1)
                if 3 in parts and not (first and par == 0):
                    act_e.wait_ge(carry_saved, n)
                for w in range(3):
                    if 3 + w in parts:
                        full(3 + w)
                        act_e.activation(pre[:, w * BC:(w + 1) * BC, TAPS - 1:],
                                         banks[:, ring[3 + w], :].rearrange("p (a t) -> p a t", a=BC), ACT.Copy
                                         ).then_inc(proj_free, 1)
                if 6 in parts:
                    if not first:
                        act_e.wait_ge(qkv_stored[par], 64 * idx)
                    full(6)
                    act_e.activation(beta_sb[:, par, :, :],
                                     banks[0:H, ring[6], 0:2 * P].rearrange("p (b t) -> p b t", b=2), ACT.Sigmoid
                                     ).then_inc(proj_free, 1)
                for w in range(3):
                    if 7 + w in parts:
                        full(7 + w)
                        act_e.activation(act[:, par, w, :, :],
                                         banks[:, ring[7 + w], :].rearrange("p (a t) -> p a t", a=BC),
                                         ACT.Silu).then_inc(proj_free, 1)

            def fwd_bank(name):
                return banks[:, BANK[name], :]

            def masked_q(par, j):
                for i in range(4):
                    h = (j % 2) * 4 + i
                    last = act_e.activation(qm[:, j % 2, i, :], q_f[:, par, j // 2, :], ACT.Copy,
                                            scale=block_ones[:, h * D:h * D + 1])
                last.then_inc(qm_ready, 1)

            def queries(idx, par):
                act_e.wait_ge(f_loaded[par], 16 * F_DMAS * (idx + 1))
                act_e.activation(qsq, q_f[:, par, :, :].rearrange("p a t -> p (a t)"), ACT.Square).then_inc(qsq_ready, 1)
                masked_q(par, 0)
                masked_q(par, 1)

            def writes(idx, par):
                act_e.wait_ge(fwd_full, FWD * idx + AT[f"u{par}"] + 1)
                act_e.activation(u_pad.rearrange("p a (h x) -> p a h x", x=PAD)[:, :, :, 0:D],
                                 fwd_bank(f"u{par}").rearrange("p (a h m) -> p a h m", a=BC, h=HB), ACT.Copy
                                 ).then_inc(fwd_free, 1)
                act_e.wait_ge(att_full, ATT * (2 * idx + par) + 1)
                act_e.activation(guard[:, :], banks[:, 6, :], ACT.Relu, scale=RMS_EPS * D, bias=least[:, 0:1]
                                 ).then_inc(att_free, 1)

            def grams(idx, par, which):
                for j in which:
                    act_e.wait_ge(att_full, ATT * (2 * idx + par) + j + 2)
                    act_e.activation(pm[:, j % 2, :, :], banks[:, 6 + (1 + j) % 2, :].rearrange("p (h t) -> p h t", h=4),
                                     ACT.Copy).then_inc(att_free, 1)
                    if j + 2 < GRAMS:
                        masked_q(par, j + 2)

            def answers(idx, par):
                act_e.wait_ge(fwd_full, FWD * idx + AT[f"o{par}"] + 1)
                act_e.activation(osq[:, :], fwd_bank(f"o{par}"), ACT.Square)
                act_e.activation(o_f[:, par, :, :, :].rearrange("p b a t -> p (b a t)"), fwd_bank(f"o{par}"), ACT.Copy
                                 ).then_inc(fwd_free, 1)

            def mean_square(idx, par):
                act_e.wait_ge(att_full, ATT * (2 * idx + par + 1))
                act_e.activation(scale_f[:, par, :], banks[:, 6 + (ATT - 1) % 2, :], ACT.Copy).then_inc(att_free, 1)

            def norm(idx, par):
                act_e.wait_ge(square_ready, 2 * idx + par + 1)
                act_e.activation(scale_f[:, par, :], scale_f[:, par, :], ACT.Sqrt, bias=least[:, 1:2]).then_inc(norm_root, 1)

            def forward(idx, par, parts):
                def full(k):
                    act_e.wait_ge(fwd_full, FWD * idx + AT[MAIN[par][k]] + 1)

                def bank(k):
                    return fwd_bank(MAIN[par][k])

                if 0 in parts:
                    full(0)
                    act_e.activation(x2T[:, par, :, :, :].rearrange("p b a t -> p (b a t)"), bank(0), ACT.Copy
                                     ).then_inc(fwd_free, 1)
                if 1 in parts:
                    full(1)
                    for a in range(CB):
                        last = act_e.activation(zT[:, :, a, :],
                                                bank(1).rearrange("p (b a t) -> p b a t", b=2, a=CB)[:, :, a, :],
                                                ACT.Identity, bias=b2col[:, a:a + 1])
                    last.then_inc(fwd_free, 1)
                for k in range(FB // 2):
                    if 2 + k in parts:
                        full(2 + k)
                        act_e.activation(hid[:, 2 * k:2 * k + 2, :, :].rearrange("p f b t -> p (f b t)"), bank(2 + k),
                                         ACT.Relu).then_inc(fwd_free, 1)
                if 6 in parts:
                    full(6)
                    act_e.activation(drive[:, par, :], bank(6), ACT.Copy).then_inc(fwd_free, 1)

            def forward_tail(idx, par, first):
                act_e.wait_ge(fwd_full, FWD * idx + AT[f"t{par}"] + 1)
                if not first:
                    act_e.wait_ge(out_stored[par], 16 * idx)
                act_e.activation(out_sb[:, par, :, :].rearrange("p b c -> p (b c)"), fwd_bank(f"t{par}"), ACT.Copy
                                 ).then_inc(fwd_free, 1)

            def root_next(s):
                act_e.wait_ge(*window_here(s))
                act_e.sem_inc(act_turns, 1)
                b = beta_w[:, bass.ds(s % 2, 1), :]
                act_e.activation(b, b, ACT.Sqrt)
                act_e.wait_ge(ss_ready, s + 1)
                act_e.activation(root[:, :], ss[:, :], ACT.Sqrt).then_inc(root_ready, 1)

            act_e.wait_ge(setup_free, JOBS)
            act_e.wait_ge(c_loaded, 16 * (6 + HB))
            for idx in range(LEAD):
                for par in range(2):
                    project(idx, par, first=(idx == 0))
                if idx == 1:
                    root_next(0)
                    for j, job_ in enumerate(late_jobs):
                        transposed(j, job_, 4 + j % 4, late_full, late_free)
            root_next(1)

            use, chunk = 0, 0
            for a in range(CB):
                for oq in range(OG // OQ):
                    if chunk >= 2:
                        act_e.wait_ge(map_stored[chunk % 2], 16 * (chunk // 2))
                    for k in range(OQ):
                        act_e.wait_ge(map_full, use + 1)
                        act_e.activation(map_st[:, chunk % 2, :, k, :],
                                         banks[:, 4 + use % 4, :].rearrange("p (o b) -> p b o", o=OPG), ACT.Copy
                                         ).then_inc(map_free, 1)
                        use += 1
                    chunk += 1
            project(LEAD, 0, range(2))
            act_e.wait_ge(pad_ready, 2)
            act_e.wait_ge(block_ready, 3)
            act_e.wait_ge(const_ready, 3)

            for first, last, flags in SEGMENTS:
                with slots(act_e, first, last) as s:
                    nxt, idx = s + LEAD, s - FOLLOW
                    p, f = "p" in flags, "f" in flags
                    if p:
                        project(nxt, 0, range(2, PROJ - 1))
                    if f:
                        queries(idx, 0)
                    if p:
                        project(nxt, 0, [PROJ - 1])
                    if "t" in flags:
                        for par in range(2):
                            forward_tail(idx - 1, par, first == FIRST_T)
                    if p:
                        project(nxt, 1, [0])
                    if f:
                        writes(idx, 0)
                    if p:
                        project(nxt, 1, [1])
                    if f:
                        grams(idx, 0, range(0, 2))
                    if p:
                        project(nxt, 1, [2])
                    if f:
                        grams(idx, 0, range(2, 6))
                    if p:
                        project(nxt, 1, [3, 4, 5, 6])
                    if f:
                        grams(idx, 0, range(6, GRAMS))
                        answers(idx, 0)
                    if p:
                        project(nxt, 1, [7])
                    if f:
                        mean_square(idx, 0)
                        queries(idx, 1)
                        norm(idx, 0)
                    if "n" in flags:
                        root_next(s + 1)
                    if p:
                        project(nxt, 1, [8, 9])
                    if f:
                        writes(idx, 1)
                        grams(idx, 1, range(0, 6))
                        forward(idx, 0, [0])
                        grams(idx, 1, range(6, GRAMS))
                        forward(idx, 0, [1])
                        answers(idx, 1)
                        forward(idx, 0, [2, 3])
                        mean_square(idx, 1)
                        forward(idx, 0, [4])
                        norm(idx, 1)
                        forward(idx, 0, [5, 6])
                        forward(idx, 1, [0])
                    if "x" in flags:
                        project(nxt + 1, 0, [0])
                    if f:
                        forward(idx, 1, [1])
                    if "x" in flags:
                        project(nxt + 1, 0, [1])
                    if f:
                        forward(idx, 1, range(2, 7))

        @block.tensor
        def _(pe):
            pe.wait_ge(ident_ready, 1)
            pe.wait_ge(w_loaded, 16 * 8)

            def transpose_weight(j, blocks, bank, full, free):
                if j >= 4:
                    pe.wait_ge(free, j - 3)
                at = 0
                for b in blocks:
                    rows = b.shape[0]
                    last = pe.transpose(banks[:, bank, at:at + rows], b, ident[0:rows, 0:rows])
                    at += rows
                last.then_inc(full, 1)

            for j, (blocks, _, _) in enumerate(jobs):
                transpose_weight(j, blocks, j % 4, setup_full, setup_free)
            pe.wait_ge(setup_free, JOBS - 4)
            pe.wait_ge(wide_ready, 1)
            pe.matmul(banks[:, (JOBS - 1) % 4, 0:B], cond_wide[:, :, :].rearrange("b e r -> b (e r)"),
                      ident[0:B, 0:B], start=True, stop=True).then_inc(setup_full, 1)
            pe.wait_ge(setup_free, JOBS)
            pe.wait_ge(diag_ready, 3 * CB * TAPS)

            def project(idx, par, parts=range(PROJ), first=False):
                n = 2 * idx + par
                ring = [k % 2 for k in range(PROJ)]

                def free(k):
                    if not (first and PROJ * par + k < 2):
                        pe.wait_ge(proj_free, PROJ * n + k - 1)

                def read(k):
                    pe.wait_ge(proj_free, PROJ * n + k + 1)

                def bank(k):
                    return banks[:, ring[k], :].rearrange("p (b a t) -> p b a t", b=2, a=CB)

                if 0 in parts:
                    pe.wait_ge(x_loaded[par], 16 * (idx + 1))
                    free(0)
                    for b in range(2):
                        for a in range(CB):
                            last = pe.transpose(bank(0)[:, b, a, :], x_tok[:, par, b, a * P:(a + 1) * P], ident[:, :])
                    last.then_inc(proj_full, 1)
                if 1 in parts:
                    free(1)
                    read(0)
                    for c in range(CB):
                        last = pe.matmul(banks[:, ring[1], 0:2 * P], AsT[:, c, :], xT[:, :, c, :],
                                         start=(c == 0), stop=(c == CB - 1))
                    last.then_inc(proj_full, 1)
                if 2 in parts:
                    free(2)
                    for a in range(CB):
                        for c in range(CB):
                            pe.matmul(bank(2)[:, :, a, :], WbaseT[:, c, a * P:(a + 1) * P], xT[:, :, c, :],
                                      start=(c == 0), stop=False)
                        if a == 0:
                            read(1)
                        last = pe.matmul(bank(2)[:, :, a, :], BsT[:, a * P:(a + 1) * P], loraT[:, :, :],
                                         start=False, stop=True)
                    last.then_inc(proj_full, 1)
                if 3 in parts:
                    read(2)
                for w in range(3):
                    if 3 + w in parts:
                        free(3 + w)
                        for a in range(CB):
                            for c in range(CB):
                                last = pe.matmul(bank(3 + w)[:, :, a, :], WqkvT[:, w, c, a * P:(a + 1) * P], yT[:, :, c, :],
                                                 start=(c == 0), stop=(c == CB - 1))
                        last.then_inc(proj_full, 1)
                if 6 in parts:
                    free(6)
                    for c in range(CB):
                        last = pe.matmul(banks[0:H, ring[6], 0:2 * P], WbT[:, c, :], yT[:, :, c, :],
                                         start=(c == 0), stop=(c == CB - 1))
                    last.then_inc(proj_full, 1)
                for w in range(3):
                    if 7 + w in parts:
                        free(7 + w)
                        read(3 + w)
                        if w == 0:
                            pe.wait_ge(head_ready, n + 1)
                        for a in range(CB):
                            for k in range(TAPS):
                                last = pe.matmul(bank(7 + w)[:, :, a, :], diag[:, w, a, k, :],
                                                 pre[:, w * BC:(w + 1) * BC, k:k + P].rearrange(
                                                     "p (b a) t -> p b a t", a=CB)[:, :, a, :],
                                                 start=(k == 0), stop=(k == TAPS - 1))
                        last.then_inc(proj_full, 1)

            def fwd_bank(name):
                return banks[:, BANK[name], :].rearrange("p (b a t) -> p b a t", b=2, a=CB)

            def fwd_turn(idx, name, first):
                if not (first and before(name) < 0):
                    pe.wait_ge(fwd_free, FWD * idx + before(name) + 1)

            def att_turn(n, i, first):
                if not (first and i < 2):
                    pe.wait_ge(att_free, ATT * n + i - 1)

            def writes(idx, par, first):
                n = 2 * idx + par
                pe.wait_ge(f_loaded[par], 16 * F_DMAS * (idx + 1))
                fwd_turn(idx, f"u{par}", first)
                for bc in range(BC):
                    last = pe.transpose(banks[:, BANK[f"u{par}"], bc * P:(bc + 1) * P], u_f[:, par, bc, :], ident[:, :])
                last.then_inc(fwd_full, 1)
                att_turn(n, 0, first and par == 0)
                pe.wait_ge(qsq_ready, n + 1)
                pe.matmul(banks[:, 6, :], block_ones[:, :], qsq, start=True, stop=True).then_inc(att_full, 1)

            def gram(idx, par, j, first=False):
                n = 2 * idx + par
                att_turn(n, 1 + j, first and par == 0)
                pe.wait_ge(qm_ready, GRAMS * n + j + 1)
                pe.matmul(banks[:, 6 + (1 + j) % 2, :], k_f[:, par, j // 2, :], qm[:, j % 2, :, :],
                          start=True, stop=True).then_inc(att_full, 1)

            def answers(idx, par, which, first=False):
                n = 2 * idx + par
                if 0 in which:
                    fwd_turn(idx, f"o{par}", first)
                    pe.wait_ge(fwd_free, FWD * idx + AT[f"u{par}"] + 1)
                    pe.wait_ge(s0_ready, n + 1)
                for j in which:
                    bc, hh = j // 2, j % 2
                    o = banks[:, BANK[f"o{par}"], bc * P:(bc + 1) * P]
                    pe.wait_ge(pm_ready, GRAMS * n + j + 1)
                    for i in range(4):
                        h = hh * 4 + i
                        pe.matmul(o, u_pad[:, bc, h * P:(h + 1) * P], pm[:, j % 2, i, :], start=(h == 0), stop=False,
                                  skip_group_check=True)
                    if hh == 1:
                        last = pe.matmul(o, s0_block[:, bc, :, :].rearrange("p h m -> p (h m)"), q_f[:, par, bc, :],
                                         start=False, stop=True, skip_group_check=True)
                    if j == GRAMS - 1:
                        last.then_inc(fwd_full, 1)
                    if j + 2 < GRAMS:
                        gram(idx, par, j + 2)

            def mean_square(idx, par):
                att_turn(2 * idx + par, ATT - 1, False)
                pe.wait_ge(fwd_free, FWD * idx + AT[f"o{par}"] + 1)
                pe.matmul(banks[:, 6 + (ATT - 1) % 2, :], block_mean[:, :], osq[:, :], start=True, stop=True
                          ).then_inc(att_full, 1)

            def forward(idx, par, parts, first=False):
                n = 2 * idx + par

                def turn(k):
                    fwd_turn(idx, MAIN[par][k], first)

                def read(k):
                    pe.wait_ge(fwd_free, FWD * idx + AT[MAIN[par][k]] + 1)

                def bank(k):
                    return fwd_bank(MAIN[par][k])

                if 0 in parts:
                    turn(0)
                    pe.wait_ge(o_ready, n + 1)
                    for a in range(CB):
                        for c in range(CB):
                            pe.matmul(bank(0)[:, :, a, :], WoT[:, c, a * P:(a + 1) * P], o_f[:, par, :, c, :],
                                      start=(c == 0), stop=False, skip_group_check=True)
                        for b in range(2):
                            last = pe.matmul(bank(0)[:, b, a, :], xf_tok[:, par, b, a * P:(a + 1) * P], ident[:, :],
                                             start=False, stop=True, skip_group_check=True)
                    last.then_inc(fwd_full, 1)
                if 1 in parts:
                    turn(1)
                    read(0)
                    for b in range(2):
                        for a in range(CB):
                            for c in range(CB):
                                last = pe.matmul(bank(1)[:, b, a, :], mapb[:, par, b * CB + c, a * P:(a + 1) * P],
                                                 x2T[:, par, b, c, :], start=(c == 0), stop=(c == CB - 1))
                    last.then_inc(fwd_full, 1)
                if 2 in parts:
                    read(1)
                for k in range(FB // 2):
                    if 2 + k in parts:
                        turn(2 + k)
                        for a in range(2):
                            f = 2 * k + a
                            for c in range(CB):
                                last = pe.matmul(banks[:, BANK[MAIN[par][2 + k]], a * 2 * P:(a + 1) * 2 * P],
                                                 WfcT[:, c, f * P:(f + 1) * P], zT[:, :, c, :],
                                                 start=(c == 0), stop=(c == CB - 1))
                        last.then_inc(fwd_full, 1)
                if 6 in parts:
                    turn(6)
                    for a in range(CB):
                        for f in range(FB):
                            if a == 0 and f % 2 == 0:
                                pe.wait_ge(hid_squared, (FB // 2) * n + f // 2 + 1)
                            last = pe.matmul(bank(6)[:, :, a, :], WprojT[:, f, a * P:(a + 1) * P], hid[:, f, :, :],
                                             start=(f == 0), stop=(f == FB - 1))
                    last.then_inc(fwd_full, 1)

            def forward_tail(idx, par):
                fwd_turn(idx, f"t{par}", False)
                pe.wait_ge(total_ready[par], idx + 1)
                for b in range(2):
                    for a in range(CB):
                        last = pe.transpose(fwd_bank(f"t{par}")[:, b, a, :], total[:, par, b, a, :], ident[:, :])
                last.then_inc(fwd_full, 1)

            for idx in range(LEAD):
                for par in range(2):
                    project(idx, par, first=(idx == 0))
                if idx == 1:
                    pe.wait_ge(late_loaded, 16 * 3)
                    for j, (blocks, _, _) in enumerate(late_jobs):
                        transpose_weight(j, blocks, 4 + j % 4, late_full, late_free)
            pe.wait_ge(late_free, len(late_jobs))

            pe.wait_ge(map_masked, 1)
            pe.wait_ge(pick_ready, 1)
            use = 0
            for a in range(CB):
                for og in range(OG):
                    if use >= 4:
                        pe.wait_ge(map_free, use - 3)
                    pe.matmul(banks[:, 4 + use % 4, :], map_w[:, og, a * P:(a + 1) * P], pick_cond[:, :, :],
                              start=True, stop=True).then_inc(map_full, 1)
                    use += 1
            pe.wait_ge(map_free, use)
            pe.wait_ge(block_ready, 3)
            project(LEAD, 0, range(2))

            for first, last_, flags in SEGMENTS:
                with slots(pe, first, last_) as s:
                    nxt, idx = s + LEAD, s - FOLLOW
                    p, f, start = "p" in flags, "f" in flags, first == FIRST_F
                    if p:
                        project(nxt, 0, range(2, PROJ))
                    if "t" in flags:
                        for par in range(2):
                            forward_tail(idx - 1, par)
                    if p:
                        project(nxt, 1, [0])
                    if f:
                        writes(idx, 0, start)
                    if p:
                        project(nxt, 1, [1])
                    if f:
                        gram(idx, 0, 0, start)
                        gram(idx, 0, 1, start)
                    if p:
                        project(nxt, 1, [2])
                    if f:
                        answers(idx, 0, range(0, 4), start)
                    if p:
                        project(nxt, 1, [3, 4, 5, 6])
                    if f:
                        answers(idx, 0, range(4, GRAMS))
                    if p:
                        project(nxt, 1, [7])
                    if f:
                        mean_square(idx, 0)
                    if p:
                        project(nxt, 1, [8, 9])
                    if f:
                        writes(idx, 1, start)
                        gram(idx, 1, 0)
                        gram(idx, 1, 1)
                        answers(idx, 1, range(0, 4))
                        forward(idx, 0, [0], start)
                        answers(idx, 1, range(4, 6))
                        forward(idx, 0, [1], start)
                        answers(idx, 1, range(6, GRAMS))
                        forward(idx, 0, [2, 3], start)
                        mean_square(idx, 1)
                        forward(idx, 0, [4, 5, 6])
                        forward(idx, 1, [0])
                    if "x" in flags:
                        project(nxt + 1, 0, [0])
                    if f:
                        forward(idx, 1, [1])
                    if "x" in flags:
                        project(nxt + 1, 0, [1])
                    if f:
                        forward(idx, 1, range(2, 7))


INS = ['x', 'cond_8', 'L0_cond_W_base', 'L0_cond_b_base', 'L0_cond_As', 'L0_cond_Bs', 'L0_attn_Wq', 'L0_attn_Wk',
       'L0_attn_Wv', 'L0_attn_Wb', 'L0_attn_Wo', 'L0_attn_conv_q', 'L0_attn_conv_k', 'L0_attn_conv_v',
       'L0_attn_o_norm_w', 'L0_cond2_weight', 'L0_cond2_mask', 'L0_cond2_bias', 'L0_ffn_W_fc', 'L0_ffn_W_proj']


def kernel(**inputs):
    import numpy as _np
    import concourse.bacc as _bacc
    from concourse import mybir as _mybir
    from concourse.bass_utils import run_bass_kernel_spmd as _run

    nc = _bacc.Bacc("TRN2", target_bir_lowering=False, num_devices=1)
    arrays, args = {}, []
    for name in INS:
        a = _np.ascontiguousarray(inputs[name])
        arrays[f"in_{name}"] = a
        args.append(nc.dram_tensor(f"in_{name}", a.shape, _mybir.dt.from_np(a.dtype), kind="ExternalInput").ap())
    out = nc.dram_tensor("out", inputs["x"].shape, _mybir.dt.float32, kind="ExternalOutput").ap()
    adaln_attention_ffn(nc, *args, out)
    r = _run(nc, [arrays], core_ids=[0])
    return r.results[0]["out"]
```
